# Optimizing a Trainium2 kernel written in Bass

```python
import numpy as np
import jax
import jax.numpy as jnp

def _softmax(x, axis=-1):
    return jax.nn.softmax(x, axis=axis)

def _gelu(x):
    return jax.nn.gelu(x, approximate=True)

def _silu(x):
    return jax.nn.silu(x)

def _sigmoid(x):
    return jax.nn.sigmoid(x)

def _layernorm(x, axis=-1, eps=1e-05):
    m = jnp.mean(x, axis=axis, keepdims=True)
    v = jnp.var(x, axis=axis, keepdims=True)
    return (x - m) / jnp.sqrt(v + eps)

def _scatter_add(tgt, idx, src, axis=0):
    return tgt.at[idx].add(src)

def _segment_sum(src, seg, n):
    return jax.ops.segment_sum(src, seg, n)
kernel_name = 'mk_adaln_d1_jaxref_r4_11f3d8'

def setup_inputs(seed: int=0):
    np.random.seed(seed)
    _w = jnp.asarray

    def _L0_attn_setup():
        import jax, jax.numpy as jnp
        import numpy as np
        H = 16
        D_MODEL = 512
        HEAD_DIM = D_MODEL // H
        B, S = (4, 512)
        key = jax.random.key(seed)
        ks = jax.random.split(key, 9)
        std = D_MODEL ** (-0.5)
        hidden_states = jax.random.normal(ks[0], (B, S, D_MODEL), dtype=jnp.float32)
        q_w = jax.random.normal(ks[1], (H * HEAD_DIM, D_MODEL), dtype=jnp.float32) * std
        k_w = jax.random.normal(ks[2], (HEAD_DIM, D_MODEL), dtype=jnp.float32) * std
        v_w = jax.random.normal(ks[3], (HEAD_DIM, D_MODEL), dtype=jnp.float32) * std
        o_w = jax.random.normal(ks[4], (D_MODEL, H * HEAD_DIM), dtype=jnp.float32) * std
        q_b = jnp.zeros((H * HEAD_DIM,), dtype=jnp.float32)
        k_b = jnp.zeros((HEAD_DIM,), dtype=jnp.float32)
        v_b = jnp.zeros((HEAD_DIM,), dtype=jnp.float32)
        o_b = jnp.zeros((D_MODEL,), dtype=jnp.float32)
        return {'hidden_states': hidden_states, 'q_w': q_w, 'q_b': q_b, 'k_w': k_w, 'k_b': k_b, 'v_w': v_w, 'v_b': v_b, 'o_w': o_w, 'o_b': o_b}
    _L0_attn_in = _L0_attn_setup()

    def _L0_ffn_setup():
        import jax, jax.numpy as jnp
        import numpy as np
        HIDDEN = 512
        INTER = 2048
        SCALE = 64.0

        def fwht(x):
            orig_shape = x.shape
            n = orig_shape[-1]
            x = x.reshape(-1, n)
            h = 1
            while h < n:
                x = x.reshape(-1, n // (2 * h), 2, h)
                a, b = (x[:, :, 0, :], x[:, :, 1, :])
                x = jnp.stack([a + b, a - b], axis=2).reshape(-1, n)
                h *= 2
            return (x / jnp.sqrt(jnp.asarray(n, x.dtype))).reshape(orig_shape)
        key = jax.random.key(seed)
        ks = jax.random.split(key, 8)
        inp = jax.random.normal(ks[0], (4, 512, HIDDEN), dtype=jnp.float32)
        SU_ug = jnp.where(jax.random.bernoulli(ks[1], 0.5, (HIDDEN,)), 1.0, -1.0).astype(jnp.float32)
        SU_dp = jnp.where(jax.random.bernoulli(ks[2], 0.5, (INTER,)), 1.0, -1.0).astype(jnp.float32)
        Wscale_ug = jax.random.uniform(ks[3], (2 * INTER,), jnp.float32, 0.5, 1.5)
        Wscale_dp = jax.random.uniform(ks[4], (HIDDEN,), jnp.float32, 0.5, 1.5)
        W_up = jax.random.normal(ks[5], (INTER, HIDDEN), dtype=jnp.float32) * 0.02
        W_gate = jax.random.normal(ks[6], (INTER, HIDDEN), dtype=jnp.float32) * 0.02
        W_down = jax.random.normal(ks[7], (HIDDEN, INTER), dtype=jnp.float32) * 0.02
        return {'input': inp, 'SU_ug': SU_ug, 'SU_dp': SU_dp, 'Wscale_ug': Wscale_ug, 'Wscale_dp': Wscale_dp, 'W_up': W_up, 'W_gate': W_gate, 'W_down': W_down}
    _L0_ffn_in = _L0_ffn_setup()
    _L0_c = _w((lambda *s: np.random.randn(*s).astype(np.float32) * 0.05)(4, 512))
    _L0_wmod = _w((lambda *s: np.random.randn(*s).astype(np.float32) * 0.05)(512, 6 * 512) * 512 ** (-0.5))
    _d = {'L0_attn_hidden_states': _L0_attn_in['hidden_states'], 'L0_attn_q_w': _L0_attn_in['q_w'], 'L0_attn_q_b': _L0_attn_in['q_b'], 'L0_attn_k_w': _L0_attn_in['k_w'], 'L0_attn_k_b': _L0_attn_in['k_b'], 'L0_attn_v_w': _L0_attn_in['v_w'], 'L0_attn_v_b': _L0_attn_in['v_b'], 'L0_attn_o_w': _L0_attn_in['o_w'], 'L0_attn_o_b': _L0_attn_in['o_b'], 'L0_ffn_SU_ug': _L0_ffn_in['SU_ug'], 'L0_ffn_SU_dp': _L0_ffn_in['SU_dp'], 'L0_ffn_Wscale_ug': _L0_ffn_in['Wscale_ug'], 'L0_ffn_Wscale_dp': _L0_ffn_in['Wscale_dp'], 'L0_ffn_W_up': _L0_ffn_in['W_up'], 'L0_ffn_W_gate': _L0_ffn_in['W_gate'], 'L0_ffn_W_down': _L0_ffn_in['W_down'], 'L0_c': _L0_c, 'L0_wmod': _L0_wmod}
    _x0 = _d['L0_attn_hidden_states']
    _d['L0_attn_hidden_states'] = jax.random.normal(jax.random.fold_in(jax.random.key(seed), 1), (4, 1024, 512), dtype=_x0.dtype)
    del _x0
    return _d

def reference(L0_attn_hidden_states, L0_attn_q_w, L0_attn_q_b, L0_attn_k_w, L0_attn_k_b, L0_attn_v_w, L0_attn_v_b, L0_attn_o_w, L0_attn_o_b, L0_ffn_SU_ug, L0_ffn_SU_dp, L0_ffn_Wscale_ug, L0_ffn_Wscale_dp, L0_ffn_W_up, L0_ffn_W_gate, L0_ffn_W_down, L0_c, L0_wmod):

    def _L0_attn_ref(hidden_states, q_w, q_b, k_w, k_b, v_w, v_b, o_w, o_b):
        import jax, jax.numpy as jnp
        import numpy as np
        H = 16
        D_MODEL = 512
        HEAD_DIM = D_MODEL // H
        B, S = (4, 512)
        b, s, _ = hidden_states.shape
        q = (hidden_states @ q_w.T + q_b).reshape(b, s, H, HEAD_DIM)
        k = hidden_states @ k_w.T + k_b
        v = hidden_states @ v_w.T + v_b
        scores = jnp.einsum('bqhd,bkd->bhqk', q, k) / HEAD_DIM ** 0.5
        causal = jnp.triu(jnp.ones((s, s), dtype=bool), k=1)
        scores = jnp.where(causal[None, None], -jnp.inf, scores)
        attn = jax.nn.softmax(scores.astype(jnp.float32), axis=-1).astype(q.dtype)
        out = jnp.einsum('bhqk,bkd->bqhd', attn, v).reshape(b, s, H * HEAD_DIM)
        return out @ o_w.T + o_b

    def _L0_ffn_ref(input, SU_ug, SU_dp, Wscale_ug, Wscale_dp, W_up, W_gate, W_down):
        import jax, jax.numpy as jnp
        import numpy as np
        HIDDEN = 512
        INTER = 2048
        SCALE = 64.0

        def fwht(x):
            orig_shape = x.shape
            n = orig_shape[-1]
            x = x.reshape(-1, n)
            h = 1
            while h < n:
                x = x.reshape(-1, n // (2 * h), 2, h)
                a, b = (x[:, :, 0, :], x[:, :, 1, :])
                x = jnp.stack([a + b, a - b], axis=2).reshape(-1, n)
                h *= 2
            return (x / jnp.sqrt(jnp.asarray(n, x.dtype))).reshape(orig_shape)
        n = SU_ug.shape[0]
        x = input.reshape(-1, n)
        x = fwht(x * SU_ug) / SCALE
        x_up = x @ W_up.T * (Wscale_ug[:INTER] * SCALE)
        x_gate = x @ W_gate.T * (Wscale_ug[INTER:] * SCALE)
        x = jax.nn.silu(x_gate) * x_up
        x = fwht(x * SU_dp) / SCALE
        x = x @ W_down.T * (Wscale_dp * SCALE)
        return x.reshape(input.shape)
    x = L0_attn_hidden_states
    mod = (_silu(L0_c) @ L0_wmod).reshape(L0_c.shape[0], 6, 1, -1)
    sa, ca, ga, sb, cb, gb = (mod[:, 0], mod[:, 1], mod[:, 2], mod[:, 3], mod[:, 4], mod[:, 5])
    ga = (2 * (ga >= 0) - 1) * jnp.maximum(jnp.abs(ga), 0.25)
    gb = (2 * (gb >= 0) - 1) * jnp.maximum(jnp.abs(gb), 0.25)
    h = _layernorm(x, axis=-1) * (1 + ca) + sa
    x = x + ga * _L0_attn_ref(h, L0_attn_q_w, L0_attn_q_b, L0_attn_k_w, L0_attn_k_b, L0_attn_v_w, L0_attn_v_b, L0_attn_o_w, L0_attn_o_b)
    h = _layernorm(x, axis=-1) * (1 + cb) + sb
    x = x + gb * _L0_ffn_ref(h, L0_ffn_SU_ug, L0_ffn_SU_dp, L0_ffn_Wscale_ug, L0_ffn_Wscale_dp, L0_ffn_W_up, L0_ffn_W_gate, L0_ffn_W_down)
    return x

_drawn_inputs = setup_inputs


def setup_inputs(seed=0):
    import zlib

    import numpy as np

    out = dict(_drawn_inputs(seed))
    spreads = {'L0_attn_q_b': (0.0, 0.8),
     'L0_attn_k_b': (0.0, 0.8),
     'L0_attn_v_b': (0.0, 0.343),
     'L0_attn_o_b': (0.0, 0.312)}
    factors = {'L0_ffn_Wscale_ug': 5.083, 'L0_ffn_Wscale_dp': 7.478}
    for name, (base, spread) in spreads.items():
        noise = np.random.default_rng([zlib.crc32(name.encode()), seed]).standard_normal(out[name].shape)
        drawn = base * np.exp(spread * noise) if base else spread * noise
        out[name] = jnp.asarray(drawn.astype(out[name].dtype))
    for name, factor in factors.items():
        out[name] = (out[name] * factor).astype(out[name].dtype)
    return out
```

```python
import concourse.bass as bass
from concourse import mybir
from contextlib import ExitStack

F32 = mybir.dt.float32
F32R = mybir.dt.float32r
ALU = mybir.AluOpType
ACT = mybir.ActivationFunctionType
AX = mybir.AxisListType

P = 128
D = 512
KT = D // P
HEADS = 16
HD = D // HEADS
GROUPS = KT
FF = 2048
FT = FF // P
HALF = 512
SCALE = HD ** -0.5
EPS = 1e-5
BIG = 2.0 ** 100

UNITS = [
    (0, [(0, 0, 512, 0), (1, 128, 384, 512)]),
    (0, [(2, 256, 256, 0), (3, 384, 128, 256)]),
    (1, [(0, 512, 512, 0), (1, 512, 512, 512)]),
    (1, [(2, 512, 512, 0), (3, 512, 512, 512)]),
    (1, [(4, 512, 512, 0), (5, 640, 384, 512)]),
    (1, [(6, 768, 256, 0), (7, 896, 128, 256)]),
]
SLOTS = [
    [(0, 0, 128, 0), (1, 0, 256, 128)], [(2, 0, 384, 0)], [(3, 0, 512, 0)],
    [(4, 0, 512, 0)], [(4, 512, 128, 0)], [(5, 0, 512, 0)], [(5, 512, 256, 0)],
    [(6, 0, 512, 0)], [(6, 512, 384, 0)], [(7, 0, 512, 0)], [(7, 512, 512, 0)],
]
NS = len(SLOTS) + 1

SIDE_KV = 0
SIDE_Q0 = 2
SIDE_HEAD0 = 4
SIDE_STEP0 = SIDE_HEAD0 + 2 * NS
SIDE_LOOP = SIDE_STEP0 + NS
SIDE_PER_GROUP = 2 + 4 * NS
SIDE_TAIL = SIDE_LOOP + 3 * SIDE_PER_GROUP
SIDE_OUT = SIDE_TAIL + NS
SIDE_ALL = SIDE_OUT + 8


class Chain:

    def __init__(self, engine, sem):
        self.engine, self.sem, self.base, self.n = engine, sem, 0, 0

    def link(self, instruction):
        self.n += 1
        instruction.then_inc(self.sem, 1)
        self.engine.wait_ge(self.sem, self.base + self.n)

    def loop(self, register, per_pass):
        outer = (self.base, self.n, per_pass)
        self.base, self.n = self.base + self.n + register * per_pass, 0
        return outer

    def end(self, outer, passes):
        assert self.n == outer[2], (self.n, outer)
        self.base, self.n = outer[0], outer[1] + passes * outer[2]


def program(nc, io, B, S):
    TT = S // P
    assert S == 2 * HALF and TT == 8
    x1_dram = nc.dram_tensor("x1_dram", (B, TT, P, D), F32).ap()
    qw_dram = nc.dram_tensor("qw_split_dram", (GROUPS + 1, P, 2, KT, P), F32).ap()
    ctx = ExitStack()
    with ctx:
        def sem(name):
            return ctx.enter_context(nc.semaphore(name))

        def sb(stack, name, shape, dt=F32):
            return stack.enter_context(nc.sbuf_tensor(name, shape, dt))

        bank = [ctx.enter_context(nc.psum_tensor(f"bank{n}", [P, 2, HALF], F32)) for n in range(4)]
        ident = sb(ctx, "ident", [P, P])
        mod = sb(ctx, "mod", [P, 4, KT, B])
        eps = sb(ctx, "eps", [P, 1])
        with ExitStack() as attention:
            T = dict(
                ow=sb(attention, "ow_split", [P, 2, KT, D], F32R),
                kvw=sb(attention, "kvw_split", [P, 2, KT, P], F32R),
                identr=sb(attention, "identr", [P, P], F32R),
                mask_kq=sb(attention, "mask_kq", [P, P], F32R),
                mask_qk=sb(attention, "mask_qk", [P, P], F32R),
                kvb=sb(attention, "kvb", [P, 1]),
                ga=sb(attention, "ga", [P, B, D]), ob=sb(attention, "ob_split", [2, D], F32R), ones=sb(attention, "ones2", [2, P], F32R),
                kst=sb(attention, "k_stack", [98, S], F32R),
                vs=sb(attention, "v_ones", [P, TT, 2 * HD]),
            )
            with ExitStack() as temps:
                attention_setup(nc, io, B, sem, lambda *a: sb(temps, *a), bank, ident, mod, eps, T, qw_dram)
            attention_phase(nc, io, B, S, sem, lambda *a: sb(attention, *a), bank, ident, mod, eps, T, qw_dram, x1_dram)
        with ExitStack() as ffn:
            W = dict(
                ug=sb(ffn, "w_upgate", [P, KT, 2, FF]), d=sb(ffn, "w_down", [P, FT, D]),
                sug=sb(ffn, "scale_upgate", [P, 2, FT]), gbw=sb(ffn, "gbw", [P, B, D]),
            )
            with ExitStack() as temps:
                ffn_setup(nc, io, B, sem, lambda *a: sb(temps, *a), bank, W)
            ffn_phase(nc, io, B, S, sem, lambda *a: sb(ffn, *a), bank, ident, mod, eps, W, x1_dram)


def attention_setup(nc, io, B, sem, sb, bank, ident, mod, eps, T, qw_dram):
    wm = sb("wmod_sb", [P, 5, KT, D])
    ct = sb("c_t", [P, KT, B])
    cs = sb("c_silu", [P, KT, B])
    cbc = sb("c_bcast", [P, KT, B, P])
    qraw = sb("qw_raw", [P, KT, D])
    qsp = sb("qw_split", [P, 2, KT, D], F32R)
    oraw = sb("ow_raw", [P, KT, D])
    kvraw = sb("kvw_raw", [P, KT, P])
    obr, obs, ones = sb("ob_raw", [1, D]), sb("ob_hi_lo", [1, 2, D], F32R), sb("ones", [2, P])
    mk = sb("masks", [P, 2, P])
    fl = sb("floor_tmp", [P, 3, D])
    c_in, wm_in, w_in, bias_in = sem("c_in"), [sem(f"wmod_in{n}") for n in range(5)], sem("attn_w_in"), sem("attn_bias_in")
    const_step, const_ready = sem("const_step"), sem("const_ready")
    silu_done, cbc_ready, mod_done, g_done, g_free = sem("silu_c_done"), sem("cbc_ready"), sem("mod_done"), sem("ga_done"), sem("ga_free")
    dve_step, split_ready, qw_out, ob_split = sem("setup_dve_step"), sem("qw_split_ready"), sem("qw_out"), sem("ob_split")

    with nc.Block() as block:
        @block.sync
        def _(sp):
            sp.dma_start(ct[:], io["cT"]).then_inc(c_in, 16)
            wmv = io["wmod"].rearrange("(k p) (m n) -> m p k n", p=P, n=D)
            for n, m in enumerate((0, 1, 2, 3, 4)):
                sp.dma_start(wm[:, n, :, :], wmv[m]).then_inc(wm_in[n], 16)
            sp.dma_start(qraw[:], io["qwT"].rearrange("(k p) n -> p k n", p=P)).then_inc(w_in, 16)
            sp.dma_start(oraw[:], io["owT"].rearrange("(k p) n -> p k n", p=P)).then_inc(w_in, 16)
            for r in range(3):
                sp.dma_start(kvraw[:, :, r * HD:(r + 1) * HD], io["kwT"].rearrange("(k p) n -> p k n", p=P)).then_inc(w_in, 16)
                sp.dma_start(T["kvb"][r * HD:(r + 1) * HD, :], io["kb"]).then_inc(bias_in, 16)
            sp.dma_start(kvraw[:, :, 96:P], io["vwT"].rearrange("(k p) n -> p k n", p=P)).then_inc(w_in, 16)
            sp.dma_start(T["kvb"][96:P, :], io["vb"]).then_inc(bias_in, 16)
            sp.dma_start(obr[:], io["ob"]).then_inc(bias_in, 16)
            sp.wait_ge(split_ready, 1)
            for g in range(GROUPS + 1):
                at = g % GROUPS * P
                sp.dma_start(qw_dram[g], qsp[:, :, :, at:at + P].bitcast(F32)).then_inc(qw_out, 16)
            sp.wait_ge(qw_out, 16 * (GROUPS + 1))
            sp.wait_ge(ob_split, 1)
            for part in range(2):
                sp.dma_start(T["ob"][part:part + 1, :].bitcast(F32), obs[:, part, :].bitcast(F32)).then_inc(qw_out, 16)
            sp.wait_ge(qw_out, 16 * (GROUPS + 3))

        @block.gpsimd
        def _(pool):
            nc.gpsimd.memset(ident[:], 0.0).then_inc(const_step, 1)
            nc.gpsimd.memset(mk[:], 0.0).then_inc(const_step, 1)
            pool.wait_ge(const_step, 2)
            nc.gpsimd.affine_select(out=ident[:], in_=ident[:], compare_op=ALU.not_equal, fill=1.0, base=0,
                                    pattern=[[-1, P]], channel_multiplier=1).then_inc(const_ready, 1)
            nc.gpsimd.affine_select(out=mk[:, 0, :], in_=mk[:, 0, :], compare_op=ALU.is_ge, fill=-BIG, base=0,
                                    pattern=[[1, P]], channel_multiplier=-1).then_inc(const_ready, 1)
            nc.gpsimd.affine_select(out=mk[:, 1, :], in_=mk[:, 1, :], compare_op=ALU.is_ge, fill=-BIG, base=0,
                                    pattern=[[-1, P]], channel_multiplier=1).then_inc(const_ready, 1)

        @block.scalar
        def _(act):
            act.wait_ge(c_in, 16)
            nc.scalar.activation(cs[:], ct[:], ACT.Silu).then_inc(silu_done, 1)

        @block.tensor
        def _(pe):
            pe.wait_ge(silu_done, 1)
            for n, m in enumerate((0, 1, 3, 4)):
                pe.wait_ge(wm_in[m], 16)
                for o in range(KT):
                    for k in range(KT):
                        last = nc.tensor.matmul(bank[0][:, 0, (n * KT + o) * B:(n * KT + o + 1) * B],
                                                wm[:, m, k, o * P:(o + 1) * P], cs[:, k, :],
                                                start=(k == 0), stop=(k == KT - 1))
            last.then_inc(mod_done, 1)
            pe.wait_ge(cbc_ready, 1)
            pe.wait_ge(wm_in[2], 16)
            for b in range(B):
                if b >= 2:
                    pe.wait_ge(g_free, b - 1)
                for k in range(KT):
                    last = nc.tensor.matmul(bank[1][:, b % 2, :], cbc[:, k, b, :], wm[:, 2, k, :],
                                            start=(k == 0), stop=(k == KT - 1))
                last.then_inc(g_done, 1)

        @block.vector
        def _(dve):
            chain = Chain(dve, dve_step)
            nc.vector.memset(T["kst"][96:98, :].bitcast(F32), 1.0)
            nc.vector.memset(T["vs"][:, :, HD:2 * HD], 1.0)
            chain.link(nc.vector.memset(ones[:], 1.0))
            nc.vector.tensor_copy(T["ones"][:], ones[:])
            dve.wait_ge(silu_done, 1)
            nc.vector.tensor_copy(cbc[:], cs[:].unsqueeze(3).to_broadcast([P, KT, B, P])).then_inc(cbc_ready, 1)
            dve.wait_ge(w_in, 96)
            chain.link(nc.vector.tensor_copy(qsp[:, 0], qraw[:]))
            nc.vector.tensor_tensor(qsp[:, 1], qraw[:], qsp[:, 0].bitcast(F32), ALU.subtract).then_inc(split_ready, 1)
            chain.link(nc.vector.tensor_copy(T["ow"][:, 0], oraw[:]))
            nc.vector.tensor_tensor(T["ow"][:, 1], oraw[:], T["ow"][:, 0].bitcast(F32), ALU.subtract)
            chain.link(nc.vector.tensor_copy(T["kvw"][:, 0], kvraw[:]))
            nc.vector.tensor_tensor(T["kvw"][:, 1], kvraw[:], T["kvw"][:, 0].bitcast(F32), ALU.subtract)
            dve.wait_ge(const_ready, 3)
            nc.vector.tensor_copy(T["identr"][:], ident[:])
            nc.vector.tensor_copy(T["mask_kq"][:], mk[:, 0, :])
            nc.vector.tensor_copy(T["mask_qk"][:], mk[:, 1, :])
            dve.wait_ge(mod_done, 1)
            src = bank[0][:, 0, 0:4 * KT * B].rearrange("p (m k b) -> p m k b", m=4, k=KT)
            for m, one in enumerate((0.0, 1.0, 0.0, 1.0)):
                nc.vector.tensor_scalar(mod[:, m], src[:, m], one, None, ALU.add)
            dve.wait_ge(bias_in, 80)
            chain.link(nc.vector.tensor_copy(obs[:, 0, :], obr[:]))
            nc.vector.tensor_tensor(obs[:, 1, :], obr[:], obs[:, 0, :].bitcast(F32), ALU.subtract).then_inc(ob_split, 1)
            for b in range(B):
                dve.wait_ge(g_done, b + 1)
                floored(nc, chain, T["ga"][:, b, :], bank[1][:, b % 2, :], fl, g_free, b + 1)


def floored(nc, chain, out, psum, tmp, free, count):
    nc.vector.tensor_copy(tmp[:, 0, :], psum).then_inc(free, 1)
    chain.engine.wait_ge(free, count)
    chain.link(nc.vector.tensor_scalar(tmp[:, 2, :], tmp[:, 0, :], 0.0, 2.0, ALU.is_ge, ALU.mult))
    nc.vector.tensor_scalar(tmp[:, 2, :], tmp[:, 2, :], 1.0, None, ALU.subtract)
    chain.link(nc.vector.scalar_tensor_tensor(out=tmp[:, 1, :], in0=tmp[:, 0, :], scalar=-1.0, in1=tmp[:, 0, :],
                                              op0=ALU.mult, op1=ALU.max))
    chain.link(nc.vector.scalar_tensor_tensor(out=out, in0=tmp[:, 1, :], scalar=0.25, in1=tmp[:, 2, :],
                                              op0=ALU.max, op1=ALU.mult))


def attention_phase(nc, io, B, S, sem, sb, bank, ident, mod, eps, T, qw_dram, x1_dram):
    TT = S // P
    scores, side, obank = (bank[0], bank[1]), bank[2], bank[3]
    ow, kvw, identr, kst, vs = T["ow"], T["kvw"], T["identr"], T["kst"], T["vs"]
    x = sb("x", [P, TT, D])
    modb = sb("mod_batch", [P, 2, KT, 1])
    xn = sb("x_normed", [P, 2, D])
    ht = sb("h_t_split", [P, 2, KT, S], F32R)
    pr = sb("probs", [P, 3, S])
    hs = pr[:].rearrange("p a b -> p (a b)")[:, 0:KT * HALF].rearrange("p (k t) -> p k t", k=KT)
    qw = sb("qw_group", [P, 2, KT, P], F32R)
    q, qb = sb("q", [P, S]), sb("qb_group", [P, 1])
    qs = sb("q_split", [P, 2, S], F32R)
    qst = sb("q_stacks", [98, 4, S], F32R)
    kv = sb("kv", [P, S])
    m1, m2 = sb("max_first", [P, 8]), sb("max_second", [P, 4])
    nm = sb("neg_max", [P, 2 * 8], F32R)
    mr = sb("neg_max_rows", [16, 4, P], F32R)
    oraw = sb("o_raw", [64, S])
    og = sb("o_group", [P, 2, S])
    ot = sb("o_split", [P, 2, KT, S], F32R)
    x1 = sb("x1_out", [P, 2, D])
    tmp = sb("x1_tmp", [P, 2, D])
    st6, mv, rs = sb("ln_stats", [P, TT, 6]), sb("ln_mean_var", [P, TT, 2]), sb("ln_rstd", [P, 2, TT])

    x_in = [sem(f"x_in{t}") for t in range(TT)]
    x1_ready = sem("x1_ready")
    x1_out = [sem(f"x1_out{n}") for n in range(2)]
    stats_ready, sd_ready, xn_ready, xt_done, h_ready, ht_ready = (
        sem(n) for n in ("stats_ready", "sd_ready", "xn_ready", "xt_done", "h_ready", "ht_ready"))
    kst_ready, vt_done, vs_ready = sem("kst_ready"), sem("vt_done"), sem("vs_ready")
    qw_in, qs_ready = sem("qw_in"), sem("qs_ready")
    q_loaded = [sem(f"q_loaded{n}") for n in range(4)]
    m_loaded = [sem(f"m_loaded{n}") for n in range(4)]
    side_full, side_free = [sem("side_full0"), sem("side_full1")], [sem("side_free0"), sem("side_free1")]
    nm_ready, scored, exped = sem("nm_ready"), sem("scored"), sem("exped")
    pv_done, o_free = sem("pv_done"), [sem("o_free0"), sem("o_free1")]
    gathered, group_normed = sem("gathered"), sem("group_normed")
    dve_step = sem("attn_dve_step")
    NU = len(UNITS)

    def side_use(b, n, g=0):
        return n % 2, b * (SIDE_ALL // 2) + n // 2 + g * (SIDE_PER_GROUP // 2)

    def side_of_max(n):
        if n < 2:
            return SIDE_HEAD0 + n * NS
        if n == 2:
            return SIDE_STEP0
        return SIDE_LOOP + 2 + (n - 3) * NS if n < 7 else SIDE_TAIL

    def side_taken(engine, b, n, g=0):
        r, use = side_use(b, n, g)
        engine.wait_ge(side_free[r], use + 1)

    def queries_taken(engine, b, group, g):
        for h in range(2):
            side_taken(engine, b, (SIDE_Q0 if isinstance(group, int) and group == 0 else SIDE_LOOP) + h, g)

    with nc.Block() as block:
        @block.sync
        def _(sp):
            def fetch_group(group):
                sp.dma_start(qw[:].bitcast(F32), qw_dram[group]).then_inc(qw_in, 16)
                sp.dma_start(qb[:], io["qb"][group]).then_inc(qw_in, 16)

            def load_stack(b, n, g, group):
                s = n % 4
                sp.wait_ge(scored, (b * HEADS + 4 * g + n - 3) * NU if n >= 3 else b * HEADS * NU)
                sp.wait_ge(qs_ready, b * GROUPS + group + 1)
                for part, of in enumerate((0, 0, 1)):
                    sp.dma_start(qst[part * HD:(part + 1) * HD, s, :].bitcast(F32), qs[s * HD:(s + 1) * HD, of, :].bitcast(F32)).then_inc(q_loaded[s], 16)

            def load_max(b, n, g):
                s = n % 4
                side_taken(sp, b, side_of_max(n) + NS - 1, g)
                sp.dma_start(qst[96:98, s, :].bitcast(F32).rearrange("r (t q) -> r t q", q=P), mr[:, s, :].bitcast(F32)).then_inc(m_loaded[s], 16)

            def gather(b, n, g):
                j = n % 4
                for c in range(2):
                    sp.wait_ge(o_free[c], b * HEADS + 4 * g + n + 1)
                for part in range(2):
                    sp.dma_start(og[j * HD:(j + 1) * HD, part, :], oraw[part * HD:(part + 1) * HD, :]).then_inc(gathered, 16)

            def step(b, n, g, has_load, has_max):
                if has_load:
                    load_stack(b, n + 3, g, g + (n + 3) // 4)
                gather(b, n, g)
                if has_max:
                    load_max(b, n + 2, g)

            fetch_group(0)
            with sp.Fori(0, B) as b:
                for n in range(3):
                    load_stack(b, n, 0, 0)
                for n in range(2):
                    load_max(b, n, 0)
                queries_taken(sp, b, 0, 0)
                fetch_group(1)
                step(b, 0, 0, True, True)
                with sp.Fori(0, 3) as g:
                    for n in range(1, 5):
                        if n == 2:
                            queries_taken(sp, b, g + 1, g)
                            fetch_group(g + 2)
                        step(b, n, g, True, True)
                for n in range(13, 16):
                    step(b, n, 0, False, n == 13)
                for t in range(TT):
                    sp.wait_ge(x1_ready, (b + 1) * TT + t + 1)
                    sp.dma_start(x1_dram[b, t], x1[:, t % 2, :]).then_inc(x1_out[t % 2], 16)
            for n in range(2):
                sp.wait_ge(x1_out[n], 16 * B * TT // 2)
            sp.wait_ge(qw_in, 32 * (B * GROUPS + 1))

        @block.scalar
        def _(act):
            def side_copy(b, n, g, out, bias, rows=P, width=HALF):
                r, use = side_use(b, n, g)
                act.wait_ge(side_full[r], use + 1)
                if bias is None:
                    ins = nc.scalar.activation(out, side[0:rows, r, 0:width], ACT.Copy)
                else:
                    ins = nc.scalar.activation(out, side[0:rows, r, 0:width], ACT.Identity, bias=bias)
                ins.then_inc(side_free[r], 1)

            def queries(b, g, first):
                for h in range(2):
                    side_copy(b, first + h, g, q[:, h * HALF:(h + 1) * HALF], qb[:])

            def max_rows(b, n, g):
                side_copy(b, side_of_max(n) + NS - 1, g, mr[:, n % 4, :], None, rows=16, width=P)

            def evacuate(b, n, g, c):
                head = b * HEADS + 4 * g + n
                act.wait_ge(pv_done, head * NU + (2, NU)[c])
                if c == 0:
                    act.wait_ge(gathered, 32 * head)
                elif n % 4 == 0:
                    act.wait_ge(group_normed, b * GROUPS + g + n // 4)
                nc.scalar.activation(oraw[:, c * HALF:(c + 1) * HALF], obank[0:64, c, :], ACT.Copy).then_inc(o_free[c], 1)

            def step(b, n, g, has_q, has_max):
                if has_q:
                    queries(b, g, SIDE_LOOP)
                for u, (c, parts) in enumerate(UNITS):
                    unit = (b * HEADS + 4 * g + n) * NU + u
                    width = sum(p[2] for p in parts)
                    act.wait_ge(scored, unit + 1)
                    if n > 0 or u >= 3:
                        act.wait_ge(pv_done, unit - 2)
                    nc.scalar.activation(pr[:, u % 3, 0:width], scores[u % 2][:].rearrange("p a b -> p (a b)")[:, 0:width],
                                         ACT.Exp, scale=SCALE).then_inc(exped, 1)
                    if u == 3:
                        evacuate(b, n, g, 0)
                evacuate(b, n, g, 1)
                if has_max:
                    max_rows(b, n + 2, g)

            with act.Fori(0, B) as b:
                for t in range(TT):
                    act.wait_ge(x1_ready, b * TT + t + 1)
                    act.dma_start(x[:, t, :], io["x"][b, t]).then_inc(x_in[t], 16)
                nc.scalar.activation(modb[:], mod[:, 0:2, :, bass.ds(b, 1)], ACT.Copy)
                act.wait_ge(stats_ready, b + 1)
                nc.scalar.activation(rs[:, 0, :], mv[:, :, 1], ACT.Sqrt, bias=eps[:]).then_inc(sd_ready, 1)
                for h in range(2):
                    act.wait_ge(xt_done, b * TT + 4 * (h + 1))
                    for k in range(KT):
                        if h:
                            act.wait_ge(ht_ready, b * 2 * KT + k + 1)
                        nc.scalar.activation(hs[:, k, :], scores[k // 2][:, k % 2, :], ACT.Identity,
                                             bias=modb[:, 0, k, :], scale=modb[:, 1, k, :]).then_inc(h_ready, 1)
                for h in range(2):
                    side_copy(b, SIDE_KV + h, 0, kv[:, h * HALF:(h + 1) * HALF], T["kvb"][:])
                queries(b, 0, SIDE_Q0)
                max_rows(b, 0, 0)
                act.wait_ge(vt_done, b + 1)
                nc.scalar.activation(vs[:, :, 0:HD], obank[:, 0, 0:TT * HD].rearrange("p (t d) -> p t d", t=TT), ACT.Copy).then_inc(vs_ready, 1)
                max_rows(b, 1, 0)
                step(b, 0, 0, False, True)
                with act.Fori(0, 3) as g:
                    for n in range(1, 5):
                        step(b, n, g, n == 1, True)
                for n in range(13, 16):
                    step(b, n, 0, False, n == 13)

        @block.vector
        def _(dve):
            chain = Chain(dve, dve_step)
            nc.vector.memset(tmp[:, 0, :], 0.0).then_inc(x1_ready, TT)

            def maxima(b, n, g):
                for i, slot in enumerate(SLOTS):
                    r, use = side_use(b, side_of_max(n) + i, g)
                    dve.wait_ge(side_full[r], use + 1)
                    for qt, k0, w, col in slot:
                        out = m1[:, qt:qt + 1] if k0 == 0 else m2[:, qt - 4:qt - 3]
                        last = nc.vector.tensor_reduce(out, side[:, r, col:col + w], AX.X, ALU.max)
                    last.then_inc(side_free[r], 1)
                for i in (NS - 3, NS - 2):
                    side_taken(dve, b, side_of_max(n) + i, g)
                chain.link(nc.vector.tensor_tensor(m1[:, 4:8], m1[:, 4:8], m2[:], ALU.max))
                if n > 0:
                    r, use = side_use(b, side_of_max(n) - (3 if n == 3 else 1), g)
                    dve.wait_ge(side_full[r], use + 1)
                chain.link(nc.vector.tensor_scalar(nm[:, 0:8], m1[:], -1.0, None, ALU.mult))
                nc.vector.scalar_tensor_tensor(out=nm[:, 8:16], in0=m1[:], scalar=-1.0, in1=nm[:, 0:8].bitcast(F32),
                                               op0=ALU.mult, op1=ALU.subtract).then_inc(nm_ready, 1)

            def split_queries(b, group, g):
                queries_taken(dve, b, group, g)
                dve.wait_ge(q_loaded[3], 48 * (b * GROUPS + group))
                chain.link(nc.vector.tensor_copy(qs[:, 0, :], q[:]))
                nc.vector.tensor_tensor(qs[:, 1, :], q[:], qs[:, 0, :].bitcast(F32), ALU.subtract).then_inc(qs_ready, 1)

            def normalise(b, group, out_at):
                dve.wait_ge(gathered, 32 * (b * HEADS + 4 * (group + 1)))
                chain.link(nc.vector.reciprocal(og[:, 1, :], og[:, 1, :]))
                chain.link(nc.vector.tensor_tensor(og[:, 0, :], og[:, 0, :], og[:, 1, :], ALU.mult))
                chain.link(nc.vector.tensor_copy(out_at(0), og[:, 0, :]))
                nc.vector.tensor_tensor(out_at(1), og[:, 0, :], out_at(0).bitcast(F32), ALU.subtract).then_inc(group_normed, 1)

            def step(b, n, g, has_q, has_max, has_norm):
                if has_q:
                    split_queries(b, g + 1, g)
                if has_max:
                    maxima(b, n + 2, g)
                if has_norm:
                    normalise(b, g, lambda part: ot[:, part, g, :])

            with dve.Fori(0, B) as b:
                outer = chain.loop(b, 59)
                for t in range(TT):
                    dve.wait_ge(x_in[t], 16 * (b + 1))
                    last = nc.vector.bn_stats(st6[:, t, :], x[:, t, :])
                chain.link(last)
                nc.vector.memset(eps[:], EPS)
                for t in range(TT):
                    last = nc.vector.bn_aggr(mv[:, t, :], st6[:, t, :])
                last.then_inc(stats_ready, 1)
                dve.wait_ge(sd_ready, b + 1)
                chain.link(nc.vector.reciprocal(rs[:, 1, :], rs[:, 0, :]))

                def normed(t):
                    if t >= 2:
                        dve.wait_ge(xt_done, b * TT + t - 1)
                    nc.vector.tensor_scalar(xn[:, t % 2, :], x[:, t, :], mv[:, t, 0:1], rs[:, 1, t:t + 1],
                                            ALU.subtract, ALU.mult).then_inc(xn_ready, 1)

                def split_h(h):
                    at = slice(h * HALF, (h + 1) * HALF)
                    for k in range(KT):
                        dve.wait_ge(h_ready, b * 2 * KT + h * KT + k + 1)
                        chain.link(nc.vector.tensor_copy(ht[:, 0, k, at], hs[:, k, :]))
                        nc.vector.tensor_tensor(ht[:, 1, k, at], hs[:, k, :], ht[:, 0, k, at].bitcast(F32),
                                                ALU.subtract).then_inc(ht_ready, 1)
                for t in range(6):
                    normed(t)
                split_h(0)
                for t in range(6, 8):
                    normed(t)
                split_h(1)
                for h in range(2):
                    side_taken(dve, b, SIDE_KV + h)
                chain.link(nc.vector.tensor_copy(kst[0:96, :], kv[0:96, :]))
                nc.vector.tensor_tensor(kst[32:64, :], kv[32:64, :], kst[32:64, :].bitcast(F32), ALU.subtract).then_inc(kst_ready, 1)
                split_queries(b, 0, 0)
                for n in range(2):
                    maxima(b, n, 0)
                step(b, 0, 0, False, True, False)
                with dve.Fori(0, 3) as g:
                    inner = chain.loop(g, 12)
                    for n in range(1, 5):
                        step(b, n, g, n == 1, True, n == 4)
                    chain.end(inner, 3)
                step(b, 13, 0, False, True, False)
                normalise(b, 3, lambda part: ot[:, part, 3, :])
                for t in range(TT):
                    r, use = side_use(b, SIDE_OUT + t)
                    dve.wait_ge(side_full[r], use + 1)
                    ins = nc.vector.tensor_tensor(tmp[:, t % 2, :], side[:, r, :], T["ga"][:, b, :], ALU.mult)
                    ins.then_inc(side_free[r], 1)
                    dve.wait_ge(side_free[r], use + 1)
                    dve.wait_ge(x1_out[t % 2], 16 * (b * TT // 2 + t // 2))
                    nc.vector.tensor_tensor(x1[:, t % 2, :], tmp[:, t % 2, :], x[:, t, :], ALU.add).then_inc(x1_ready, 1)
                chain.end(outer, B)

        @block.tensor
        def _(pe):
            def side_bank(b, n, g=0):
                r, use = side_use(b, n, g)
                pe.wait_ge(side_free[r], use)
                return r

            def product(out, weights, moving, kts, last=True):
                for k in range(kts):
                    for a, m in ((0, 0), (0, 1), (1, 0)):
                        ins = nc.tensor.matmul(out, weights(a, k), moving(m, k), start=(k == 0 and a + m == 0),
                                               stop=(last and k == kts - 1 and a == 1))
                return ins

            def project_q(b, g, group, first):
                pe.wait_ge(qw_in, 32 * (b * GROUPS + group + 1))
                for h in range(2):
                    r = side_bank(b, first + h, g)
                    product(side[:, r, :], lambda p, k: qw[:, p, k, :],
                            lambda p, k: ht[:, p, k, h * HALF:(h + 1) * HALF], KT).then_inc(side_full[r], 1)

            def max_slot(b, n, g, i):
                s = n % 4
                r = side_bank(b, side_of_max(n) + i, g)
                if i == NS - 1:
                    pe.wait_ge(nm_ready, b * HEADS + 4 * g + n + 1)
                    nc.tensor.transpose(side[0:16, r, 0:P], nm[:].bitcast(F32), ident[:]).then_inc(side_full[r], 1)
                    return
                if i == 0:
                    pe.wait_ge(q_loaded[s], 48 * (b * GROUPS + g + n // 4 + 1))
                for qt, k0, w, col in SLOTS[i]:
                    diagonal = k0 + w == (qt + 1) * P
                    last = nc.tensor.matmul(side[:, r, col:col + w], qst[0:96, s, qt * P:(qt + 1) * P], kst[0:96, k0:k0 + w],
                                            start=True, stop=not diagonal)
                    if diagonal:
                        last = nc.tensor.matmul(side[:, r, col + w - P:col + w], identr[:], T["mask_qk"][:],
                                                start=False, stop=True)
                last.then_inc(side_full[r], 1)

            def score(b, n, g, u):
                s = n % 4
                unit = (b * HEADS + 4 * g + n) * NU + u
                if u == 0:
                    pe.wait_ge(m_loaded[s], 16 * (b * GROUPS + g + n // 4 + 1))
                if n > 0 or u >= 2:
                    pe.wait_ge(exped, unit - 1)
                out = scores[u % 2][:].rearrange("p a b -> p (a b)")
                for kt, q0, w, col in UNITS[u][1]:
                    diagonal = q0 == kt * P
                    last = nc.tensor.matmul(out[:, col:col + w], kst[0:98, kt * P:(kt + 1) * P], qst[0:98, s, q0:q0 + w],
                                            start=True, stop=not diagonal)
                    if diagonal:
                        last = nc.tensor.matmul(out[:, col:col + P], identr[:], T["mask_kq"][:], start=False, stop=True)
                last.then_inc(scored, 1)

            def weigh(b, n, g, u):
                c, parts = UNITS[u]
                head = b * HEADS + 4 * g + n
                pe.wait_ge(exped, head * NU + u + 1)
                if parts[0][0] == 0:
                    pe.wait_ge(o_free[c], head)
                for kt, q0, w, col in parts:
                    ins = nc.tensor.matmul(obank[0:64, c, q0 - c * HALF:q0 - c * HALF + w], vs[:, kt, :], pr[:, u % 3, col:col + w],
                                           start=(kt == 0), stop=(kt == 3 + 4 * c))
                ins.then_inc(pv_done, 1)

            def step(b, n, g, has_q, has_max):
                if has_q:
                    project_q(b, g, g + 1, SIDE_LOOP)
                for u in range(NU):
                    score(b, n, g, u)
                    if u:
                        weigh(b, n, g, u - 1)
                    if has_max:
                        for i in (2 * u, 2 * u + 1):
                            if i < NS - 1:
                                max_slot(b, n + 2, g, i)
                weigh(b, n, g, NU - 1)
                if has_max:
                    max_slot(b, n + 2, g, NS - 1)

            with pe.Fori(0, B) as b:
                for t in range(TT):
                    pe.wait_ge(xn_ready, b * TT + t + 1)
                    if t == 4:
                        pe.wait_ge(h_ready, b * 2 * KT + KT)
                    for k in range(KT):
                        last = nc.tensor.transpose(scores[k // 2][:, k % 2, (t % 4) * P:(t % 4 + 1) * P],
                                                   xn[:, t % 2, k * P:(k + 1) * P], ident[:])
                    last.then_inc(xt_done, 1)
                for h in range(2):
                    pe.wait_ge(ht_ready, b * 2 * KT + (h + 1) * KT)
                    r = side_bank(b, SIDE_KV + h)
                    product(side[:, r, :], lambda p, k: kvw[:, p, k, :],
                            lambda p, k: ht[:, p, k, h * HALF:(h + 1) * HALF], KT).then_inc(side_full[r], 1)
                project_q(b, 0, 0, SIDE_Q0)
                for h in range(2):
                    side_taken(pe, b, SIDE_KV + h)
                pe.wait_ge(o_free[0], b * HEADS)
                pe.wait_ge(kst_ready, b + 1)
                for i in range(NS):
                    max_slot(b, 0, 0, i)
                for t in range(TT):
                    last = nc.tensor.transpose(obank[:, 0, t * HD:(t + 1) * HD], kv[96:P, t * P:(t + 1) * P], ident[96:P, 96:P])
                last.then_inc(vt_done, 1)
                for i in range(NS):
                    max_slot(b, 1, 0, i)
                pe.wait_ge(vs_ready, b + 1)
                step(b, 0, 0, False, True)
                with pe.Fori(0, 3) as g:
                    for n in range(1, 5):
                        step(b, n, g, n == 1, True)
                for n in range(13, 16):
                    step(b, n, 0, False, n == 13)
                for t in range(TT):
                    if t == 0:
                        pe.wait_ge(group_normed, (b + 1) * GROUPS)
                    r = side_bank(b, SIDE_OUT + t)
                    product(side[:, r, :], lambda p, k: ot[:, p, k, t * P:(t + 1) * P],
                            lambda p, k: ow[:, p, k, :], KT, last=False)
                    nc.tensor.matmul(side[:, r, :], T["ones"][:], T["ob"][:], start=False, stop=True).then_inc(side_full[r], 1)


def ffn_setup(nc, io, B, sem, sb, bank, W):
    had = sb("hadamard", [P, P])
    su = sb("signs", [P, KT + FT])
    but = sb("butterfly", [P, KT, HALF])
    wm = sb("wmod_gb", [P, KT, D])
    ct, cs, cbc = sb("c_t2", [P, KT, B]), sb("c_silu2", [P, KT, B]), sb("c_bcast2", [P, KT, B, P])
    wsd = sb("wscale_down", [P, D])
    fl = sb("floor_tmp2", [P, 3, D])
    CH = FF // HALF
    small_in, wm_in = sem("ffn_small_in"), sem("wmod_gb_in")
    ug_in, d_in = [sem(f"ug_in{n}") for n in range(2 * CH)], sem("down_in")
    silu_done, cbc_ready, g_done, g_free = sem("silu_c_done2"), sem("cbc_ready2"), sem("gb_done"), sem("gb_free")
    su_ready, crossed, folded, evacuated, dve_step = sem("su_ready"), sem("crossed"), sem("folded"), sem("evacuated"), sem("ffn_setup_step")
    down, upgate = W["d"], W["ug"]

    def chunk(c):
        return upgate[:, :, c // CH, (c % CH) * HALF:(c % CH + 1) * HALF]

    tiles = [(chunk(c)[:, k, :], su_at) for c in range(2 * CH) for k in range(KT) for su_at in (k,)]
    tiles += [(down[:, f, :], KT + f) for f in range(FT)]

    with nc.Block() as block:
        @block.sync
        def _(sp):
            sp.dma_start(had[:], io["had"]).then_inc(small_in, 16)
            sp.dma_start(su[:, 0:KT], io["su_ug"]).then_inc(small_in, 16)
            sp.dma_start(su[:, KT:], io["su_dp"]).then_inc(small_in, 16)
            sp.dma_start(W["sug"][:], io["ws_ug"]).then_inc(small_in, 16)
            sp.dma_start(ct[:], io["cT"]).then_inc(small_in, 16)
            sp.dma_start(wsd[:], io["ws_dp"].to_broadcast([P, D])).then_inc(small_in, 16)
            for c in range(2 * CH):
                src = io["w_up"] if c < CH else io["w_gate"]
                sp.dma_start(chunk(c), src.rearrange("(k p) n -> p k n", p=P)[:, :, (c % CH) * HALF:(c % CH + 1) * HALF]).then_inc(ug_in[c], 16)
            sp.dma_start(down[:], io["w_down"].rearrange("(f p) n -> p f n", p=P)).then_inc(d_in, 16)
            sp.dma_start(wm[:], io["wmod"].rearrange("(k p) n -> p k n", p=P)[:, :, 5 * D:6 * D]).then_inc(wm_in, 16)

        @block.scalar
        def _(act):
            act.wait_ge(small_in, 96)
            nc.scalar.activation(cs[:], ct[:], ACT.Silu).then_inc(silu_done, 1)
            act.wait_ge(su_ready, 1)
            for n, (at, s) in enumerate(tiles):
                act.wait_ge(folded, n + 1)
                nc.scalar.activation(at, bank[n % 4 // 2][:, n % 2, :], ACT.Copy, scale=su[:, s:s + 1]).then_inc(evacuated, 1)

        @block.tensor
        def _(pe):
            pe.wait_ge(small_in, 96)
            for n, (at, s) in enumerate(tiles):
                pe.wait_ge(crossed, n // KT + 1 if n < 2 * CH * KT else 2 * CH + 4)
                if n >= 4:
                    pe.wait_ge(evacuated, n - 3)
                nc.tensor.matmul(bank[n % 4 // 2][:, n % 2, :], had[:], at, start=True, stop=True).then_inc(folded, 1)
            pe.wait_ge(cbc_ready, 1)
            pe.wait_ge(wm_in, 16)
            for b in range(B):
                if b >= 2:
                    pe.wait_ge(g_free, b - 1)
                for k in range(KT):
                    last = nc.tensor.matmul(bank[2][:, b % 2, :], cbc[:, k, b, :], wm[:, k, :], start=(k == 0), stop=(k == KT - 1))
                last.then_inc(g_done, 1)

        @block.vector
        def _(dve):
            chain = Chain(dve, dve_step)
            dve.wait_ge(small_in, 96)
            nc.vector.tensor_scalar(su[:, 0:KT], su[:, 0:KT], float(D) ** -0.5, None, ALU.mult)
            nc.vector.tensor_scalar(su[:, KT:], su[:, KT:], float(FF) ** -0.5, None, ALU.mult).then_inc(su_ready, 1)
            dve.wait_ge(silu_done, 1)
            nc.vector.tensor_copy(cbc[:], cs[:].unsqueeze(3).to_broadcast([P, KT, B, P])).then_inc(cbc_ready, 1)
            for c in range(2 * CH):
                w = chunk(c)
                dve.wait_ge(ug_in[c], 16)
                pairs, to = w.rearrange("p (a two) n -> p a two n", two=2), but[:].rearrange("p (a two) n -> p a two n", two=2)
                nc.vector.tensor_tensor(to[:, :, 0], pairs[:, :, 0], pairs[:, :, 1], ALU.add)
                chain.link(nc.vector.tensor_tensor(to[:, :, 1], pairs[:, :, 0], pairs[:, :, 1], ALU.subtract))
                nc.vector.tensor_tensor(w[:, 0:2], but[:, 0:2], but[:, 2:4], ALU.add)
                last = nc.vector.tensor_tensor(w[:, 2:4], but[:, 0:2], but[:, 2:4], ALU.subtract)
                last.then_inc(crossed, 1)
                dve.wait_ge(crossed, c + 1)
            dve.wait_ge(d_in, 16)
            for c in range(4):
                w = down[:, :, c * P:(c + 1) * P]
                t = but[:].rearrange("p k n -> p (k n)").rearrange("p (f n) -> p f n", n=P)
                for stage, (a, z) in enumerate(((w, t), (t, w), (w, t), (t, w))):
                    h = 2 ** stage
                    i = a.rearrange("p (a two h) n -> p a two h n", two=2, h=h)
                    o = z.rearrange("p (a two h) n -> p a two h n", two=2, h=h)
                    nc.vector.tensor_tensor(o[:, :, 0], i[:, :, 0], i[:, :, 1], ALU.add)
                    last = nc.vector.tensor_tensor(o[:, :, 1], i[:, :, 0], i[:, :, 1], ALU.subtract)
                    if stage < 3:
                        chain.link(last)
                last.then_inc(crossed, 1)
                dve.wait_ge(crossed, 2 * CH + c + 1)
            for b in range(B):
                dve.wait_ge(g_done, b + 1)
                floored(nc, chain, W["gbw"][:, b, :], bank[2][:, b % 2, :], fl, g_free, b + 1)
                nc.vector.tensor_tensor(W["gbw"][:, b, :], W["gbw"][:, b, :], wsd[:], ALU.mult)


def ffn_phase(nc, io, B, S, sem, sb, bank, ident, mod, eps, W, x1_dram):
    NT = HALF // P
    up, gate, acc = bank[0], bank[1], (bank[2], bank[3])
    modb = sb("mod_batch2", [P, 2, KT, 1])
    x1 = sb("x1_in", [P, 2, NT, D])
    xn = sb("x1_normed", [P, 2, D])
    hs = sb("h2_t", [P, KT, HALF])
    ht = sb("h2_t_split", [P, 2, KT, HALF], F32R)
    wr = [[sb(f"w_ring{n}_{p}", [P, KT, 2, P], F32R) for p in range(2)] for n in range(2)]
    dr = [[sb(f"d_ring{n}_{p}", [P, D], F32R) for p in range(2)] for n in range(2)]
    sg = sb("silu_gate", [P, 2, HALF])
    y = sb("y", [P, HALF])
    ys = [sb(f"y_split{n}", [P, 2, HALF], F32R) for n in range(2)]
    out_sb, tmp = sb("out_sb", [P, 2, D]), sb("out_tmp", [P, 2, D])
    st6, mv, rs = sb("ln2_stats", [P, NT, 6]), sb("ln2_mean_var", [P, NT, 2]), sb("ln2_rstd", [P, 2, NT])

    x1_in = [sem("x1_in0"), sem("x1_in1")]
    stats_ready, sd_ready, xn_ready, xt_done, h_ready, ht_ready = (
        sem(n) for n in ("stats2_ready", "sd2_ready", "xn2_ready", "xt2_done", "h2_ready", "ht2_ready"))
    ug_cast, d_cast, ug_ready, d_ready = sem("ug_cast"), sem("d_cast"), sem("ug_ready"), sem("d_ready")
    ug_done, silu_done, y_mul, y_ready, d_done = sem("ug_done"), sem("silu_done"), sem("y_mul"), sem("y_ready"), sem("d_done")
    out_ready, stored, dve_step = sem("out_ready"), [sem("stored0"), sem("stored1")], sem("ffn_dve_step")
    PAIRS = FT // 2

    def at_tile(n):
        return n if isinstance(n, int) else bass.ds(n, 1)

    def pairs(engine, body, chain=None, per_pass=0):
        body(0, True, False)
        with engine.Fori(1, PAIRS - 1) as p:
            if chain:
                inner = chain.loop(p - 1, per_pass)
            body(p, False, False)
            if chain:
                chain.end(inner, PAIRS - 2)
        body(PAIRS - 1, False, True)

    with nc.Block() as block:
        @block.gpsimd
        def _(pool):
            with pool.Fori(0, B) as b:
                for h in range(2):
                    pool.wait_ge(out_ready, (2 * b + h + 1) * NT)
                    pool.dma_start(x1[:, h], x1_dram[b, NT * h:NT * (h + 1)].rearrange("t p n -> p t n")).then_inc(x1_in[h], 16)

        @block.sync
        def _(sp):
            with sp.Fori(0, B) as b:
                for t in range(2 * NT):
                    sp.wait_ge(out_ready, (b + 1) * 2 * NT + t + 1)
                    sp.dma_start(io["out"][b, t], out_sb[:, t % 2, :]).then_inc(stored[t % 2], 16)
            for n in range(2):
                sp.wait_ge(stored[n], 16 * B * NT)

        @block.scalar
        def _(act):
            def cast(f, s, at):
                act.wait_ge(ug_done, f)
                nc.scalar.activation(wr[s][0][:], W["ug"][:, :, :, bass.ds(at * P, P)], ACT.Copy).then_inc(ug_cast, 1)

            nc.scalar.activation(wr[0][0][:], W["ug"][:, :, :, 0:P], ACT.Copy).then_inc(ug_cast, 1)
            nc.scalar.activation(dr[0][0][:], W["d"][:, 0, :], ACT.Copy).then_inc(d_cast, 1)
            with act.Fori(0, B) as b:
                for h in range(2):
                    blk = 2 * b + h
                    nc.scalar.activation(modb[:], mod[:, 2:4, :, bass.ds(b, 1)], ACT.Copy)
                    act.wait_ge(stats_ready, blk + 1)
                    nc.scalar.activation(rs[:, 0, :], mv[:, :, 1], ACT.Sqrt, bias=eps[:]).then_inc(sd_ready, 1)
                    act.wait_ge(xt_done, (blk + 1) * NT)
                    for k in range(KT):
                        nc.scalar.activation(hs[:, k, :], bank[k // 2][:, k % 2, :], ACT.Identity,
                                             bias=modb[:, 0, k, :], scale=modb[:, 1, k, :]).then_inc(h_ready, 1)

                    def body(p, first, last):
                        for e in range(2):
                            f, s = blk * FT + 2 * p + e, e
                            at = 2 * p + e + 1 if not (last and e) else 0
                            cast(f, 1 - s, at)
                            act.wait_ge(ug_done, f + 1)
                            nc.scalar.activation(sg[:, s, :], gate[:, s, :], ACT.Silu,
                                                 scale=W["sug"][:, 1, bass.ds(2 * p + e, 1)]).then_inc(silu_done, 1)
                            act.wait_ge(d_done, f)
                            nc.scalar.activation(dr[1 - s][0][:], W["d"][:, at_tile(at), :], ACT.Copy).then_inc(d_cast, 1)
                    pairs(act, body)

        @block.vector
        def _(dve):
            chain = Chain(dve, dve_step)
            nc.vector.memset(tmp[:, 0, :], 0.0).then_inc(out_ready, 2 * NT)

            def split_ug(f, s, at):
                dve.wait_ge(ug_cast, f + 1)
                nc.vector.tensor_tensor(wr[s][1][:], W["ug"][:, :, :, bass.ds(at * P, P)], wr[s][0][:].bitcast(F32),
                                        ALU.subtract).then_inc(ug_ready, 1)

            def split_d(f, s, at):
                dve.wait_ge(d_cast, f + 1)
                nc.vector.tensor_tensor(dr[s][1][:], W["d"][:, at_tile(at), :], dr[s][0][:].bitcast(F32), ALU.subtract).then_inc(d_ready, 1)

            split_ug(0, 0, 0)
            split_d(0, 0, 0)
            with dve.Fori(0, B) as b:
                outer = chain.loop(b, 2 * (2 + KT + FT + NT))
                for h in range(2):
                    blk = 2 * b + h
                    dve.wait_ge(x1_in[h], 16 * (b + 1))
                    for t in range(NT):
                        last = nc.vector.bn_stats(st6[:, t, :], x1[:, h, t, :])
                    chain.link(last)
                    nc.vector.memset(eps[:], EPS)
                    for t in range(NT):
                        last = nc.vector.bn_aggr(mv[:, t, :], st6[:, t, :])
                    last.then_inc(stats_ready, 1)
                    dve.wait_ge(sd_ready, blk + 1)
                    chain.link(nc.vector.reciprocal(rs[:, 1, :], rs[:, 0, :]))
                    for t in range(NT):
                        if t >= 2:
                            dve.wait_ge(xt_done, blk * NT + t - 1)
                        nc.vector.tensor_scalar(xn[:, t % 2, :], x1[:, h, t, :], mv[:, t, 0:1], rs[:, 1, t:t + 1],
                                                ALU.subtract, ALU.mult).then_inc(xn_ready, 1)
                    for k in range(KT):
                        dve.wait_ge(h_ready, blk * KT + k + 1)
                        chain.link(nc.vector.tensor_copy(ht[:, 0, k, :], hs[:, k, :]))
                        nc.vector.tensor_tensor(ht[:, 1, k, :], hs[:, k, :], ht[:, 0, k, :].bitcast(F32),
                                                ALU.subtract).then_inc(ht_ready, 1)

                    def body(p, first, last):
                        for e in range(2):
                            f, s = blk * FT + 2 * p + e, e
                            at = 2 * p + e + 1 if not (last and e) else 0
                            split_ug(f + 1, 1 - s, at)
                            dve.wait_ge(y_ready, f)
                            dve.wait_ge(silu_done, f + 1)
                            ins = nc.vector.scalar_tensor_tensor(out=y[:], in0=up[:, s, :], scalar=W["sug"][:, 0, bass.ds(2 * p + e, 1)],
                                                                 in1=sg[:, s, :], op0=ALU.mult, op1=ALU.mult)
                            ins.then_inc(y_mul, 1)
                            dve.wait_ge(y_mul, f + 1)
                            if not first:
                                dve.wait_ge(d_done, f - 1)
                            chain.link(nc.vector.tensor_copy(ys[s][:, 0, :], y[:]))
                            nc.vector.tensor_tensor(ys[s][:, 1, :], y[:], ys[s][:, 0, :].bitcast(F32), ALU.subtract).then_inc(y_ready, 1)
                            split_d(f + 1, 1 - s, at)
                    pairs(dve, body, chain, 2)
                    dve.wait_ge(d_done, (blk + 1) * FT)
                    for t in range(NT):
                        chain.link(nc.vector.tensor_tensor(tmp[:, t % 2, :], acc[t // 2][:, t % 2, :], W["gbw"][:, b, :], ALU.mult))
                        dve.wait_ge(stored[t % 2], 16 * (blk * NT // 2 + t // 2))
                        ins = nc.vector.tensor_tensor(out_sb[:, t % 2, :], tmp[:, t % 2, :], x1[:, h, t, :], ALU.add)
                        ins.then_inc(out_ready, 1)
                chain.end(outer, B)

        @block.tensor
        def _(pe):
            def up_gate(f, s):
                pe.wait_ge(ug_ready, f + 1)
                for side in range(2):
                    for k in range(KT):
                        for a, m in ((0, 0), (0, 1), (1, 0)):
                            last = nc.tensor.matmul(bank[side][:, s, :], wr[s][a][:, k, side, :], ht[:, m, k, :],
                                                    start=(k == 0 and a + m == 0), stop=(k == KT - 1 and a == 1))
                last.then_inc(ug_done, 1)

            def down(f, s, first, last_one):
                pe.wait_ge(y_ready, f + 1)
                pe.wait_ge(d_ready, f + 1)
                for t in range(NT):
                    for a, m in ((0, 0), (0, 1), (1, 0)):
                        last = nc.tensor.matmul(acc[t // 2][:, t % 2, :], ys[s][:, a, t * P:(t + 1) * P], dr[s][m][:],
                                                start=(first and a + m == 0), stop=(last_one and a == 1))
                last.then_inc(d_done, 1)

            with pe.Fori(0, B) as b:
                for h in range(2):
                    blk = 2 * b + h
                    for t in range(NT):
                        pe.wait_ge(xn_ready, blk * NT + t + 1)
                        if t == 0:
                            pe.wait_ge(y_mul, blk * FT)
                        for k in range(KT):
                            last = nc.tensor.transpose(bank[k // 2][:, k % 2, t * P:(t + 1) * P],
                                                       xn[:, t % 2, k * P:(k + 1) * P], ident[:])
                        last.then_inc(xt_done, 1)
                    pe.wait_ge(ht_ready, (blk + 1) * KT)

                    def body(p, first, last):
                        f = blk * FT + 2 * p
                        for e in range(2):
                            if not first:
                                pe.wait_ge(y_mul, f + e - 1)
                            up_gate(f + e, e)
                            if e:
                                if first:
                                    pe.wait_ge(out_ready, (blk + 2) * NT)
                                down(f, 0, first, False)
                            elif not first:
                                down(f - 1, 1, False, False)
                        if last:
                            down(f + 1, 1, False, True)
                    pairs(pe, body)


def hadamard(n):
    import numpy as np
    return np.array([[1.0 - 2.0 * (bin(i & j).count("1") % 2) for j in range(n)] for i in range(n)], np.float32)


def kernel(**inputs):
    import numpy as np
    import concourse.bacc as bacc
    from concourse.bass_utils import run_bass_kernel_spmd

    a = {name.removeprefix("L0_"): np.asarray(v) for name, v in inputs.items()}
    x = a["attn_hidden_states"]
    B, S, _ = x.shape

    def lay(v):
        return np.ascontiguousarray(v)

    def columns(v):
        return lay(v.reshape(-1, P).T)

    arrays = dict(
        x=lay(x.reshape(B, S // P, P, D)),
        cT=lay(a["c"].T.reshape(KT, P, B).transpose(1, 0, 2)),
        wmod=lay(a["wmod"]),
        qwT=lay(a["attn_q_w"].T), kwT=lay(a["attn_k_w"].T), vwT=lay(a["attn_v_w"].T), owT=lay(a["attn_o_w"].T),
        qb=lay(np.concatenate([a["attn_q_b"], a["attn_q_b"][:P]]).reshape(GROUPS + 1, P, 1)), kb=lay(a["attn_k_b"].reshape(HD, 1)), vb=lay(a["attn_v_b"].reshape(HD, 1)),
        ob=lay(a["attn_o_b"].reshape(1, D)),
        su_ug=columns(a["ffn_SU_ug"]), su_dp=columns(a["ffn_SU_dp"]),
        ws_ug=lay(a["ffn_Wscale_ug"].reshape(2, FT, P).transpose(2, 0, 1)), ws_dp=lay(a["ffn_Wscale_dp"].reshape(1, D)),
        w_up=lay(a["ffn_W_up"].T), w_gate=lay(a["ffn_W_gate"].T), w_down=lay(a["ffn_W_down"].T),
        had=hadamard(P),
    )
    nc = bacc.Bacc("TRN2", target_bir_lowering=False, num_devices=1)
    io = {k: nc.dram_tensor(f"in_{k}", v.shape, mybir.dt.from_np(v.dtype), kind="ExternalInput").ap() for k, v in arrays.items()}
    io["out"] = nc.dram_tensor("out", (B, S // P, P, D), F32, kind="ExternalOutput").ap()
    program(nc, io, B, S)
    r = run_bass_kernel_spmd(nc, [{f"in_{k}": v for k, v in arrays.items()}], core_ids=[0])
    return r.results[0]["out"].reshape(B, S, D)
```

```python
import concourse.bass as bass
from concourse import mybir
from contextlib import ExitStack

F32 = mybir.dt.float32
F32R = mybir.dt.float32r
ALU = mybir.AluOpType
ACT = mybir.ActivationFunctionType
AX = mybir.AxisListType

P = 128
D = 512
KT = D // P
HEADS = 16
HD = D // HEADS
GROUPS = KT
FF = 2048
FT = FF // P
HALF = 512
SCALE = HD ** -0.5
EPS = 1e-5
BIG = 2.0 ** 100

UNITS = [
    (0, [(0, 0, 512, 0)]), (0, [(1, 128, 384, 0), (3, 384, 128, 384)]), (0, [(2, 256, 256, 0)]),
    (1, [(0, 512, 512, 0)]), (1, [(1, 512, 512, 0)]), (1, [(2, 512, 512, 0)]), (1, [(3, 512, 512, 0)]),
    (1, [(4, 512, 512, 0)]), (1, [(5, 640, 384, 0), (7, 896, 128, 384)]), (1, [(6, 768, 256, 0)]),
]
NU = len(UNITS)
C0_UNITS = sum(c == 0 for c, _ in UNITS)
RING = 4
LAG = 3
ON_POOL = [u % 5 in (0, 2, 4) for u in range(NU)]
SLOTS = [
    [(3, 0, 512, 0)], [(4, 0, 512, 0)], [(5, 0, 512, 0)], [(6, 0, 512, 0)], [(7, 0, 512, 0)], [(7, 512, 512, 0)],
    [(6, 512, 384, 0), (0, 0, 128, 384)], [(2, 0, 384, 0), (4, 512, 128, 384)], [(5, 512, 256, 0), (1, 0, 256, 256)],
]
SLOT_UNITS = [0, 0, 1, 2, 3, 4, 5, 6, 7]
NS = len(SLOTS) + 1

SIDE_KV = 0
SIDE_Q0 = 2
SIDE_HEAD0 = 4
SIDE_STEP0 = SIDE_HEAD0 + 2 * NS
SIDE_LOOP = SIDE_STEP0 + NS
SIDE_PER_GROUP = 2 + 4 * NS
SIDE_TAIL = SIDE_LOOP + 3 * SIDE_PER_GROUP
SIDE_OUT = SIDE_TAIL + NS
SIDE_ALL = SIDE_OUT + 8


class Chain:

    def __init__(self, engine, sem):
        self.engine, self.sem, self.base, self.n = engine, sem, 0, 0

    def link(self, instruction):
        self.n += 1
        instruction.then_inc(self.sem, 1)
        self.engine.wait_ge(self.sem, self.base + self.n)

    def loop(self, register, per_pass):
        outer = (self.base, self.n, per_pass)
        self.base, self.n = self.base + self.n + register * per_pass, 0
        return outer

    def end(self, outer, passes):
        assert self.n == outer[2], (self.n, outer)
        self.base, self.n = outer[0], outer[1] + passes * outer[2]


def program(nc, io, B, S):
    TT = S // P
    assert S == 2 * HALF and TT == 8
    x1_dram = nc.dram_tensor("x1_dram", (B, TT, P, D), F32).ap()
    qw_dram = nc.dram_tensor("qw_split_dram", (GROUPS + 1, P, 2, KT, P), F32).ap()
    ctx = ExitStack()
    with ctx:
        def sem(name):
            return ctx.enter_context(nc.semaphore(name))

        def sb(stack, name, shape, dt=F32):
            return stack.enter_context(nc.sbuf_tensor(name, shape, dt))

        bank = [ctx.enter_context(nc.psum_tensor(f"bank{n}", [P, 2, HALF], F32)) for n in range(4)]
        ident = sb(ctx, "ident", [P, P])
        mod = sb(ctx, "mod", [P, 4, KT, B])
        eps = sb(ctx, "eps", [P, 1])
        with ExitStack() as attention:
            T = dict(
                ow=sb(attention, "ow_split", [P, 2, KT, D], F32R),
                kvw=sb(attention, "kvw_split", [P, 2, KT, P], F32R),
                identr=sb(attention, "identr", [P, P], F32R),
                mask_kq=sb(attention, "mask_kq", [P, P], F32R),
                mask_qk=sb(attention, "mask_qk", [P, P], F32R),
                kvb=sb(attention, "kvb", [P, 1]),
                ga=sb(attention, "ga", [P, B, D]), ob=sb(attention, "ob_split", [2, D], F32R), ones=sb(attention, "ones2", [2, P], F32R),
                kst=sb(attention, "k_stack", [98, S], F32R),
                vs=sb(attention, "v_split_ones", [P, TT, 3 * HD], F32R),
            )
            with ExitStack() as temps:
                attention_setup(nc, io, B, sem, lambda *a: sb(temps, *a), bank, ident, mod, eps, T, qw_dram)
            attention_phase(nc, io, B, S, sem, lambda *a: sb(attention, *a), bank, ident, mod, eps, T, qw_dram, x1_dram)
        with ExitStack() as ffn:
            W = dict(
                ug=sb(ffn, "w_upgate", [P, KT, 2, FF]), d=sb(ffn, "w_down", [P, FT, D]),
                sug=sb(ffn, "scale_upgate", [P, 2, FT]), gbw=sb(ffn, "gbw", [P, B, D]),
            )
            with ExitStack() as temps:
                ffn_setup(nc, io, B, sem, lambda *a: sb(temps, *a), bank, W)
            ffn_phase(nc, io, B, S, sem, lambda *a: sb(ffn, *a), bank, ident, mod, eps, W, x1_dram)


def attention_setup(nc, io, B, sem, sb, bank, ident, mod, eps, T, qw_dram):
    wm = sb("wmod_sb", [P, 5, KT, D])
    ct = sb("c_t", [P, KT, B])
    cs = sb("c_silu", [P, KT, B])
    cbc = sb("c_bcast", [P, KT, B, P])
    qraw = sb("qw_raw", [P, KT, D])
    qsp = sb("qw_split", [P, 2, KT, D], F32R)
    oraw = sb("ow_raw", [P, KT, D])
    kvraw = sb("kvw_raw", [P, KT, P])
    obr, obs, ones = sb("ob_raw", [1, D]), sb("ob_hi_lo", [1, 2, D], F32R), sb("ones", [2, P])
    mk = sb("masks", [P, 2, P])
    fl = sb("floor_tmp", [P, 3, D])
    c_in, wm_in, w_in, bias_in = sem("c_in"), [sem(f"wmod_in{n}") for n in range(5)], sem("attn_w_in"), sem("attn_bias_in")
    const_step, const_ready = sem("const_step"), sem("const_ready")
    silu_done, cbc_ready, mod_done, g_done, g_free = sem("silu_c_done"), sem("cbc_ready"), sem("mod_done"), sem("ga_done"), sem("ga_free")
    dve_step, split_ready, qw_out, ob_split = sem("setup_dve_step"), sem("qw_split_ready"), sem("qw_out"), sem("ob_split")

    with nc.Block() as block:
        @block.sync
        def _(sp):
            sp.dma_start(ct[:], io["cT"]).then_inc(c_in, 16)
            wmv = io["wmod"].rearrange("(k p) (m n) -> m p k n", p=P, n=D)
            for n, m in enumerate((0, 1, 2, 3, 4)):
                sp.dma_start(wm[:, n, :, :], wmv[m]).then_inc(wm_in[n], 16)
            sp.dma_start(qraw[:], io["qwT"].rearrange("(k p) n -> p k n", p=P)).then_inc(w_in, 16)
            sp.dma_start(oraw[:], io["owT"].rearrange("(k p) n -> p k n", p=P)).then_inc(w_in, 16)
            for r in range(3):
                sp.dma_start(kvraw[:, :, r * HD:(r + 1) * HD], io["kwT"].rearrange("(k p) n -> p k n", p=P)).then_inc(w_in, 16)
                sp.dma_start(T["kvb"][r * HD:(r + 1) * HD, :], io["kb"]).then_inc(bias_in, 16)
            sp.dma_start(kvraw[:, :, 96:P], io["vwT"].rearrange("(k p) n -> p k n", p=P)).then_inc(w_in, 16)
            sp.dma_start(T["kvb"][96:P, :], io["vb"]).then_inc(bias_in, 16)
            sp.dma_start(obr[:], io["ob"]).then_inc(bias_in, 16)
            sp.wait_ge(split_ready, 1)
            for g in range(GROUPS + 1):
                at = g % GROUPS * P
                sp.dma_start(qw_dram[g], qsp[:, :, :, at:at + P].bitcast(F32)).then_inc(qw_out, 16)
            sp.wait_ge(qw_out, 16 * (GROUPS + 1))
            sp.wait_ge(ob_split, 1)
            for part in range(2):
                sp.dma_start(T["ob"][part:part + 1, :].bitcast(F32), obs[:, part, :].bitcast(F32)).then_inc(qw_out, 16)
            sp.wait_ge(qw_out, 16 * (GROUPS + 3))

        @block.gpsimd
        def _(pool):
            nc.gpsimd.memset(ident[:], 0.0).then_inc(const_step, 1)
            nc.gpsimd.memset(mk[:], 0.0).then_inc(const_step, 1)
            pool.wait_ge(const_step, 2)
            nc.gpsimd.affine_select(out=ident[:], in_=ident[:], compare_op=ALU.not_equal, fill=1.0, base=0,
                                    pattern=[[-1, P]], channel_multiplier=1).then_inc(const_ready, 1)
            nc.gpsimd.affine_select(out=mk[:, 0, :], in_=mk[:, 0, :], compare_op=ALU.is_ge, fill=-BIG, base=0,
                                    pattern=[[1, P]], channel_multiplier=-1).then_inc(const_ready, 1)
            nc.gpsimd.affine_select(out=mk[:, 1, :], in_=mk[:, 1, :], compare_op=ALU.is_ge, fill=-BIG, base=0,
                                    pattern=[[-1, P]], channel_multiplier=1).then_inc(const_ready, 1)

        @block.scalar
        def _(act):
            act.wait_ge(c_in, 16)
            nc.scalar.activation(cs[:], ct[:], ACT.Silu).then_inc(silu_done, 1)

        @block.tensor
        def _(pe):
            pe.wait_ge(silu_done, 1)
            for n, m in enumerate((0, 1, 3, 4)):
                pe.wait_ge(wm_in[m], 16)
                for o in range(KT):
                    for k in range(KT):
                        last = nc.tensor.matmul(bank[0][:, 0, (n * KT + o) * B:(n * KT + o + 1) * B],
                                                wm[:, m, k, o * P:(o + 1) * P], cs[:, k, :],
                                                start=(k == 0), stop=(k == KT - 1))
            last.then_inc(mod_done, 1)
            pe.wait_ge(cbc_ready, 1)
            pe.wait_ge(wm_in[2], 16)
            for b in range(B):
                if b >= 2:
                    pe.wait_ge(g_free, b - 1)
                for k in range(KT):
                    last = nc.tensor.matmul(bank[1][:, b % 2, :], cbc[:, k, b, :], wm[:, 2, k, :],
                                            start=(k == 0), stop=(k == KT - 1))
                last.then_inc(g_done, 1)

        @block.vector
        def _(dve):
            chain = Chain(dve, dve_step)
            nc.vector.memset(T["kst"][96:98, :].bitcast(F32), 1.0)
            nc.vector.memset(T["vs"][:, :, 2 * HD:3 * HD].bitcast(F32), 1.0)
            chain.link(nc.vector.memset(ones[:], 1.0))
            nc.vector.tensor_copy(T["ones"][:], ones[:])
            dve.wait_ge(silu_done, 1)
            nc.vector.tensor_copy(cbc[:], cs[:].unsqueeze(3).to_broadcast([P, KT, B, P])).then_inc(cbc_ready, 1)
            dve.wait_ge(w_in, 96)
            chain.link(nc.vector.tensor_copy(qsp[:, 0], qraw[:]))
            nc.vector.tensor_tensor(qsp[:, 1], qraw[:], qsp[:, 0].bitcast(F32), ALU.subtract).then_inc(split_ready, 1)
            chain.link(nc.vector.tensor_copy(T["ow"][:, 0], oraw[:]))
            nc.vector.tensor_tensor(T["ow"][:, 1], oraw[:], T["ow"][:, 0].bitcast(F32), ALU.subtract)
            chain.link(nc.vector.tensor_copy(T["kvw"][:, 0], kvraw[:]))
            nc.vector.tensor_tensor(T["kvw"][:, 1], kvraw[:], T["kvw"][:, 0].bitcast(F32), ALU.subtract)
            dve.wait_ge(const_ready, 3)
            nc.vector.tensor_copy(T["identr"][:], ident[:])
            nc.vector.tensor_copy(T["mask_kq"][:], mk[:, 0, :])
            nc.vector.tensor_copy(T["mask_qk"][:], mk[:, 1, :])
            dve.wait_ge(mod_done, 1)
            src = bank[0][:, 0, 0:4 * KT * B].rearrange("p (m k b) -> p m k b", m=4, k=KT)
            for m, one in enumerate((0.0, 1.0, 0.0, 1.0)):
                nc.vector.tensor_scalar(mod[:, m], src[:, m], one, None, ALU.add)
            dve.wait_ge(bias_in, 80)
            chain.link(nc.vector.tensor_copy(obs[:, 0, :], obr[:]))
            nc.vector.tensor_tensor(obs[:, 1, :], obr[:], obs[:, 0, :].bitcast(F32), ALU.subtract).then_inc(ob_split, 1)
            for b in range(B):
                dve.wait_ge(g_done, b + 1)
                floored(nc, chain, T["ga"][:, b, :], bank[1][:, b % 2, :], fl, g_free, b + 1)


def floored(nc, chain, out, psum, tmp, free, count):
    nc.vector.tensor_copy(tmp[:, 0, :], psum).then_inc(free, 1)
    chain.engine.wait_ge(free, count)
    chain.link(nc.vector.tensor_scalar(tmp[:, 2, :], tmp[:, 0, :], 0.0, 2.0, ALU.is_ge, ALU.mult))
    nc.vector.tensor_scalar(tmp[:, 2, :], tmp[:, 2, :], 1.0, None, ALU.subtract)
    chain.link(nc.vector.scalar_tensor_tensor(out=tmp[:, 1, :], in0=tmp[:, 0, :], scalar=-1.0, in1=tmp[:, 0, :],
                                              op0=ALU.mult, op1=ALU.max))
    chain.link(nc.vector.scalar_tensor_tensor(out=out, in0=tmp[:, 1, :], scalar=0.25, in1=tmp[:, 2, :],
                                              op0=ALU.max, op1=ALU.mult))


def attention_phase(nc, io, B, S, sem, sb, bank, ident, mod, eps, T, qw_dram, x1_dram):
    TT = S // P
    side, obank = bank[2], bank[3]

    def scores(n):
        return bank[n // 2][:, n % 2, :]

    ow, kvw, identr, kst, vs = T["ow"], T["kvw"], T["identr"], T["kst"], T["vs"]
    x = sb("x", [P, TT, D])
    modb = sb("mod_batch", [P, 2, KT, 1])
    xn = sb("x_normed", [P, 2, D])
    ht = sb("h_t_split", [P, 2, KT, S], F32R)
    pr = sb("probs", [P, RING, HALF])
    prs = [sb(f"probs_split{n}", [P, 2, HALF], F32R) for n in range(RING)]
    hs = pr[:]
    qw = sb("qw_group", [P, 2, KT, P], F32R)
    qb = sb("qb_group", [P, 1])
    qs = sb("q_split", [P, 2, S], F32R)
    qst = sb("q_stacks", [98, 4, S], F32R)
    kv = sb("kv", [P, S])
    m1, m2 = sb("max_first", [P, 8]), sb("max_second", [P, 4])
    nm = sb("neg_max", [P, 2 * 8], F32R)
    mr = sb("neg_max_rows", [16, 4, P], F32R)
    oraw = sb("o_raw", [3 * HD, S])
    og = sb("o_group", [P, 3, S])
    ot = sb("o_split", [P, 2, KT, S], F32R)
    x1 = sb("x1_out", [P, 2, D])
    tmp = sb("x1_tmp", [P, 1, D])
    st6, mv, rs = sb("ln_stats", [P, TT, 6]), sb("ln_mean_var", [P, TT, 2]), sb("ln_rstd", [P, 2, TT])

    x_in = [sem(f"x_in{t}") for t in range(TT)]
    x1_ready = sem("x1_ready")
    x1_out = [sem(f"x1_out{n}") for n in range(2)]
    stats_ready, sd_ready, xn_ready, xt_done, h_ready, ht_ready = (
        sem(n) for n in ("stats_ready", "sd_ready", "xn_ready", "xt_done", "h_ready", "ht_ready"))
    kst_ready, vt_done, vs_ready = sem("kst_ready"), sem("vt_done"), sem("vs_ready")
    qw_in, q_hi = sem("qw_in"), sem("q_hi")
    q_loaded = [sem(f"q_loaded{n}") for n in range(4)]
    m_loaded = [sem(f"m_loaded{n}") for n in range(4)]
    side_full, side_free = [sem("side_full0"), sem("side_full1")], [sem("side_free0"), sem("side_free1")]
    nm_ready, scored, exped = sem("nm_ready"), sem("scored"), sem("exped")
    lo_dve, lo_pool, o_summed, vs_lo = sem("lo_dve"), sem("lo_pool"), sem("o_summed"), sem("vs_lo")
    pv_done, o_free = sem("pv_done"), [sem("o_free0"), sem("o_free1")]
    gathered, group_normed = sem("gathered"), sem("group_normed")
    dve_step = sem("attn_dve_step")

    def lo_count(head, u, on_pool):
        return head * ON_POOL.count(on_pool) + ON_POOL[:u + 1].count(on_pool)

    def side_use(b, n, g=0):
        return n % 2, b * (SIDE_ALL // 2) + n // 2 + g * (SIDE_PER_GROUP // 2)

    def side_of_max(n):
        if n < 2:
            return SIDE_HEAD0 + n * NS
        if n == 2:
            return SIDE_STEP0
        return SIDE_LOOP + 2 + (n - 3) * NS if n < 7 else SIDE_TAIL

    def side_taken(engine, b, n, g=0):
        r, use = side_use(b, n, g)
        engine.wait_ge(side_free[r], use + 1)

    def queries_taken(engine, b, group, g):
        for h in range(2):
            side_taken(engine, b, (SIDE_Q0 if isinstance(group, int) and group == 0 else SIDE_LOOP) + h, g)

    with nc.Block() as block:
        @block.sync
        def _(sp):
            def fetch_group(group):
                sp.dma_start(qw[:].bitcast(F32), qw_dram[group]).then_inc(qw_in, 16)
                sp.dma_start(qb[:], io["qb"][group]).then_inc(qw_in, 16)

            def load_stack(b, n, g, group):
                s = n % 4
                sp.wait_ge(scored, (b * HEADS + 4 * g + n - 3) * NU if n >= 3 else b * HEADS * NU)
                queries_taken(sp, b, 0 if n <= 3 else g + 1, g)
                for part, of in enumerate((0, 0, 1)):
                    sp.dma_start(qst[part * HD:(part + 1) * HD, s, :].bitcast(F32), qs[s * HD:(s + 1) * HD, of, :].bitcast(F32)).then_inc(q_loaded[s], 16)

            def load_max(b, n, g):
                s = n % 4
                side_taken(sp, b, side_of_max(n) + NS - 1, g)
                sp.dma_start(qst[96:98, s, :].bitcast(F32).rearrange("r (t q) -> r t q", q=P), mr[:, s, :].bitcast(F32)).then_inc(m_loaded[s], 16)

            def gather(b, n, g):
                j = n % 4
                for c in range(2):
                    sp.wait_ge(o_free[c], b * HEADS + 4 * g + n + 1)
                for part in range(3):
                    sp.dma_start(og[j * HD:(j + 1) * HD, part, :], oraw[part * HD:(part + 1) * HD, :]).then_inc(gathered, 16)

            def step(b, n, g, has_load, has_max):
                if has_load:
                    load_stack(b, n + 3, g, g + (n + 3) // 4)
                gather(b, n, g)
                if has_max:
                    load_max(b, n + 2, g)

            fetch_group(0)
            with sp.Fori(0, B) as b:
                for n in range(3):
                    load_stack(b, n, 0, 0)
                for n in range(2):
                    load_max(b, n, 0)
                queries_taken(sp, b, 0, 0)
                fetch_group(1)
                step(b, 0, 0, True, True)
                with sp.Fori(0, 3) as g:
                    for n in range(1, 5):
                        if n == 2:
                            queries_taken(sp, b, g + 1, g)
                            fetch_group(g + 2)
                        step(b, n, g, True, True)
                for n in range(13, 16):
                    step(b, n, 0, False, n == 13)
                for t in range(TT):
                    sp.wait_ge(x1_ready, (b + 1) * TT + t + 1)
                    sp.dma_start(x1_dram[b, t], x1[:, t % 2, :]).then_inc(x1_out[t % 2], 16)
            for n in range(2):
                sp.wait_ge(x1_out[n], 16 * B * TT // 2)
            sp.wait_ge(qw_in, 32 * (B * GROUPS + 1))

        @block.scalar
        def _(act):
            def side_copy(b, n, g, out, bias, rows=P, width=HALF):
                r, use = side_use(b, n, g)
                act.wait_ge(side_full[r], use + 1)
                if bias is None:
                    ins = nc.scalar.activation(out, side[0:rows, r, 0:width], ACT.Copy)
                else:
                    ins = nc.scalar.activation(out, side[0:rows, r, 0:width], ACT.Identity, bias=bias)
                ins.then_inc(side_free[r], 1)

            def queries(b, group, g, first):
                for h in range(2):
                    r, use = side_use(b, first + h, g)
                    if h == 0:
                        act.wait_ge(q_loaded[3], 48 * (b * GROUPS + group))
                    act.wait_ge(side_full[r], use + 1)
                    nc.scalar.activation(qs[:, 0, h * HALF:(h + 1) * HALF], side[:, r, :], ACT.Identity, bias=qb[:]).then_inc(q_hi, 1)

            def max_rows(b, n, g):
                side_copy(b, side_of_max(n) + NS - 1, g, mr[:, n % 4, :], None, rows=16, width=P)

            def evacuate(b, n, g, c):
                head = b * HEADS + 4 * g + n
                act.wait_ge(pv_done, head * NU + (C0_UNITS, NU)[c])
                if c == 0:
                    act.wait_ge(gathered, 48 * head)
                elif n % 4 == 0:
                    act.wait_ge(group_normed, b * GROUPS + g + n // 4)
                nc.scalar.activation(oraw[:, c * HALF:(c + 1) * HALF], obank[0:3 * HD, c, :], ACT.Copy).then_inc(o_free[c], 1)

            def step(b, n, g, has_q, has_max):
                if has_q:
                    queries(b, g + 1, g, SIDE_LOOP)
                for u, (c, parts) in enumerate(UNITS):
                    unit = (b * HEADS + 4 * g + n) * NU + u
                    s = (n * NU + u) % RING
                    width = sum(p[2] for p in parts)
                    act.wait_ge(scored, unit + 1)
                    if n > 0 or u >= RING:
                        act.wait_ge(pv_done, unit - RING + 1)
                    nc.scalar.activation(pr[:, s, 0:width], scores(s)[:, 0:width], ACT.Exp, scale=SCALE)
                    nc.scalar.activation(prs[s][:, 0, 0:width], scores(s)[:, 0:width], ACT.Exp, scale=SCALE).then_inc(exped, 1)
                    if u == LAG and n > 0:
                        evacuate(b, n - 1, g, 1)
                    if u == C0_UNITS + LAG:
                        evacuate(b, n, g, 0)
                if n == 15:
                    evacuate(b, n, g, 1)
                if has_max:
                    max_rows(b, n + 2, g)

            with act.Fori(0, B) as b:
                for t in range(TT):
                    act.wait_ge(x1_ready, b * TT + t + 1)
                    act.dma_start(x[:, t, :], io["x"][b, t]).then_inc(x_in[t], 16)
                nc.scalar.activation(modb[:], mod[:, 0:2, :, bass.ds(b, 1)], ACT.Copy)
                act.wait_ge(stats_ready, b + 1)
                nc.scalar.activation(rs[:, 0, :], mv[:, :, 1], ACT.Sqrt, bias=eps[:]).then_inc(sd_ready, 1)
                for h in range(2):
                    act.wait_ge(xt_done, b * TT + 4 * (h + 1))
                    for k in range(KT):
                        if h:
                            act.wait_ge(ht_ready, b * 2 * KT + k + 1)
                        nc.scalar.activation(hs[:, k, :], scores(k), ACT.Identity,
                                             bias=modb[:, 0, k, :], scale=modb[:, 1, k, :]).then_inc(h_ready, 1)
                for h in range(2):
                    side_copy(b, SIDE_KV + h, 0, kv[:, h * HALF:(h + 1) * HALF], T["kvb"][:])
                queries(b, 0, 0, SIDE_Q0)
                max_rows(b, 0, 0)
                act.wait_ge(vt_done, b + 1)
                nc.scalar.activation(vs[:, :, 0:HD], obank[:, 0, 0:TT * HD].rearrange("p (t d) -> p t d", t=TT), ACT.Copy).then_inc(vs_ready, 1)
                max_rows(b, 1, 0)
                step(b, 0, 0, False, True)
                with act.Fori(0, 3) as g:
                    for n in range(1, 5):
                        step(b, n, g, n == 1, True)
                for n in range(13, 16):
                    step(b, n, 0, False, n == 13)

        @block.gpsimd
        def _(pool):
            def step(b, n, g, has_sum):
                for u, (c, parts) in enumerate(UNITS):
                    if ON_POOL[u]:
                        head, s, width = b * HEADS + 4 * g + n, (n * NU + u) % RING, sum(p[2] for p in parts)
                        pool.wait_ge(exped, head * NU + u + 1)
                        nc.gpsimd.tensor_tensor(prs[s][:, 1, 0:width], pr[:, s, 0:width], prs[s][:, 0, 0:width].bitcast(F32),
                                                ALU.subtract).then_inc(lo_pool, 1)
                if has_sum:
                    sum_parts(b, g)

            def sum_parts(b, group):
                pool.wait_ge(gathered, 48 * (b * HEADS + 4 * (group + 1)))
                nc.gpsimd.tensor_tensor(og[:, 0, :], og[:, 0, :], og[:, 1, :], ALU.add).then_inc(o_summed, 1)

            with pool.Fori(0, B) as b:
                step(b, 0, 0, False)
                with pool.Fori(0, 3) as g:
                    for n in range(1, 5):
                        step(b, n, g, n == 4)
                for n in range(13, 16):
                    step(b, n, 0, False)
                sum_parts(b, 3)

        @block.vector
        def _(dve):
            chain = Chain(dve, dve_step)
            nc.vector.memset(tmp[:, 0, :], 0.0).then_inc(x1_ready, TT)

            def reduce_slot(b, n, g, i):
                r, use = side_use(b, side_of_max(n) + i, g)
                dve.wait_ge(side_full[r], use + 1)
                for qt, k0, w, col in SLOTS[i]:
                    out = m1[:, qt:qt + 1] if k0 == 0 else m2[:, qt - 4:qt - 3]
                    last = nc.vector.tensor_reduce(out, side[:, r, col:col + w], AX.X, ALU.max)
                last.then_inc(side_free[r], 1)

            def merge_maxima(b, n, g):
                for i in (NS - 3, NS - 2):
                    side_taken(dve, b, side_of_max(n) + i, g)
                chain.link(nc.vector.tensor_tensor(m1[:, 4:8], m1[:, 4:8], m2[:], ALU.max))
                if n > 0:
                    r, use = side_use(b, side_of_max(n) - (3 if n == 3 else 1), g)
                    dve.wait_ge(side_full[r], use + 1)
                chain.link(nc.vector.tensor_scalar(nm[:, 0:8], m1[:], -1.0, None, ALU.mult))
                nc.vector.scalar_tensor_tensor(out=nm[:, 8:16], in0=m1[:], scalar=-1.0, in1=nm[:, 0:8].bitcast(F32),
                                               op0=ALU.mult, op1=ALU.subtract).then_inc(nm_ready, 1)

            def maxima(b, n, g):
                for i in range(len(SLOTS)):
                    reduce_slot(b, n, g, i)
                merge_maxima(b, n, g)

            def split_queries(b, group, g, first):
                for h in range(2):
                    r, use = side_use(b, first + h, g)
                    dve.wait_ge(q_hi, 2 * (b * GROUPS + group) + h + 1)
                    at = slice(h * HALF, (h + 1) * HALF)
                    nc.vector.scalar_tensor_tensor(out=qs[:, 1, at], in0=side[:, r, :], scalar=qb[:], in1=qs[:, 0, at].bitcast(F32),
                                                   op0=ALU.add, op1=ALU.subtract).then_inc(side_free[r], 1)

            def normalise(b, group, out_at):
                dve.wait_ge(gathered, 48 * (b * HEADS + 4 * (group + 1)))
                chain.link(nc.vector.reciprocal(og[:, 2, :], og[:, 2, :]))
                dve.wait_ge(o_summed, b * GROUPS + group + 1)
                chain.link(nc.vector.tensor_tensor(og[:, 0, :], og[:, 0, :], og[:, 2, :], ALU.mult))
                chain.link(nc.vector.tensor_copy(out_at(0), og[:, 0, :]))
                nc.vector.tensor_tensor(out_at(1), og[:, 0, :], out_at(0).bitcast(F32), ALU.subtract).then_inc(group_normed, 1)

            def step(b, n, g, has_q, has_max, has_norm):
                if has_q:
                    split_queries(b, g + 1, g, SIDE_LOOP)
                for u, (c, parts) in enumerate(UNITS):
                    if has_max:
                        for i, at in enumerate(SLOT_UNITS):
                            if at == u:
                                reduce_slot(b, n + 2, g, i)
                        if u == NU - 2:
                            merge_maxima(b, n + 2, g)
                    if not ON_POOL[u]:
                        head, s, width = b * HEADS + 4 * g + n, (n * NU + u) % RING, sum(p[2] for p in parts)
                        dve.wait_ge(exped, head * NU + u + 1)
                        nc.vector.tensor_tensor(prs[s][:, 1, 0:width], pr[:, s, 0:width], prs[s][:, 0, 0:width].bitcast(F32),
                                                ALU.subtract).then_inc(lo_dve, 1)
                if has_norm:
                    normalise(b, g, lambda part: ot[:, part, g, :])

            with dve.Fori(0, B) as b:
                outer = chain.loop(b, 55)
                for t in range(TT):
                    dve.wait_ge(x_in[t], 16 * (b + 1))
                    last = nc.vector.bn_stats(st6[:, t, :], x[:, t, :])
                chain.link(last)
                nc.vector.memset(eps[:], EPS)
                for t in range(TT):
                    last = nc.vector.bn_aggr(mv[:, t, :], st6[:, t, :])
                last.then_inc(stats_ready, 1)
                dve.wait_ge(sd_ready, b + 1)
                chain.link(nc.vector.reciprocal(rs[:, 1, :], rs[:, 0, :]))

                def normed(t):
                    if t >= 2:
                        dve.wait_ge(xt_done, b * TT + t - 1)
                    nc.vector.tensor_scalar(xn[:, t % 2, :], x[:, t, :], mv[:, t, 0:1], rs[:, 1, t:t + 1],
                                            ALU.subtract, ALU.mult).then_inc(xn_ready, 1)

                def split_h(h):
                    at = slice(h * HALF, (h + 1) * HALF)
                    for k in range(KT):
                        dve.wait_ge(h_ready, b * 2 * KT + h * KT + k + 1)
                        chain.link(nc.vector.tensor_copy(ht[:, 0, k, at], hs[:, k, :]))
                        nc.vector.tensor_tensor(ht[:, 1, k, at], hs[:, k, :], ht[:, 0, k, at].bitcast(F32),
                                                ALU.subtract).then_inc(ht_ready, 1)
                for t in range(6):
                    normed(t)
                split_h(0)
                for t in range(6, 8):
                    normed(t)
                split_h(1)
                for h in range(2):
                    side_taken(dve, b, SIDE_KV + h)
                chain.link(nc.vector.tensor_copy(kst[0:96, :], kv[0:96, :]))
                nc.vector.tensor_tensor(kst[32:64, :], kv[32:64, :], kst[32:64, :].bitcast(F32), ALU.subtract).then_inc(kst_ready, 1)
                split_queries(b, 0, 0, SIDE_Q0)
                maxima(b, 0, 0)
                dve.wait_ge(vs_ready, b + 1)
                nc.vector.tensor_tensor(vs[:, :, HD:2 * HD], obank[:, 0, 0:TT * HD].rearrange("p (t d) -> p t d", t=TT),
                                        vs[:, :, 0:HD].bitcast(F32), ALU.subtract).then_inc(vs_lo, 1)
                maxima(b, 1, 0)
                step(b, 0, 0, False, True, False)
                with dve.Fori(0, 3) as g:
                    inner = chain.loop(g, 11)
                    for n in range(1, 5):
                        step(b, n, g, n == 1, True, n == 4)
                    chain.end(inner, 3)
                for n in range(13, 16):
                    step(b, n, 0, False, n == 13, False)
                normalise(b, 3, lambda part: ot[:, part, 3, :])
                for t in range(TT):
                    r, use = side_use(b, SIDE_OUT + t)
                    dve.wait_ge(side_full[r], use + 1)
                    ins = nc.vector.tensor_tensor(tmp[:, 0, :], side[:, r, :], T["ga"][:, b, :], ALU.mult)
                    ins.then_inc(side_free[r], 1)
                    dve.wait_ge(side_free[r], use + 1)
                    dve.wait_ge(x1_out[t % 2], 16 * (b * TT // 2 + t // 2))
                    nc.vector.tensor_tensor(x1[:, t % 2, :], tmp[:, 0, :], x[:, t, :], ALU.add).then_inc(x1_ready, 1)
                    dve.wait_ge(x1_ready, (b + 1) * TT + t + 1)
                chain.end(outer, B)

        @block.tensor
        def _(pe):
            def side_bank(b, n, g=0):
                r, use = side_use(b, n, g)
                pe.wait_ge(side_free[r], use)
                return r

            def product(out, weights, moving, kts, last=True):
                for k in range(kts):
                    for a, m in ((0, 0), (0, 1), (1, 0)):
                        ins = nc.tensor.matmul(out, weights(a, k), moving(m, k), start=(k == 0 and a + m == 0),
                                               stop=(last and k == kts - 1 and a == 1))
                return ins

            def project_q(b, g, group, first):
                pe.wait_ge(qw_in, 32 * (b * GROUPS + group + 1))
                for h in range(2):
                    r = side_bank(b, first + h, g)
                    product(side[:, r, :], lambda p, k: qw[:, p, k, :],
                            lambda p, k: ht[:, p, k, h * HALF:(h + 1) * HALF], KT).then_inc(side_full[r], 1)

            def max_slot(b, n, g, i):
                s = n % 4
                r = side_bank(b, side_of_max(n) + i, g)
                if i == NS - 1:
                    pe.wait_ge(nm_ready, b * HEADS + 4 * g + n + 1)
                    nc.tensor.transpose(side[0:16, r, 0:P], nm[:].bitcast(F32), ident[:]).then_inc(side_full[r], 1)
                    return
                if i == 0:
                    pe.wait_ge(q_loaded[s], 48 * (b * GROUPS + g + n // 4 + 1))
                for qt, k0, w, col in SLOTS[i]:
                    diagonal = k0 + w == (qt + 1) * P
                    last = nc.tensor.matmul(side[:, r, col:col + w], qst[0:96, s, qt * P:(qt + 1) * P], kst[0:96, k0:k0 + w],
                                            start=True, stop=not diagonal)
                    if diagonal:
                        last = nc.tensor.matmul(side[:, r, col + w - P:col + w], identr[:], T["mask_qk"][:],
                                                start=False, stop=True)
                last.then_inc(side_full[r], 1)

            def score(b, n, g, u):
                s = n % 4
                unit = (b * HEADS + 4 * g + n) * NU + u
                if u == 0:
                    pe.wait_ge(m_loaded[s], 16 * (b * GROUPS + g + n // 4 + 1))
                if n > 0 or u >= RING:
                    pe.wait_ge(exped, unit - RING + 1)
                out = scores((n * NU + u) % RING)
                for kt, q0, w, col in UNITS[u][1]:
                    diagonal = q0 == kt * P
                    last = nc.tensor.matmul(out[:, col:col + w], kst[0:98, kt * P:(kt + 1) * P], qst[0:98, s, q0:q0 + w],
                                            start=True, stop=not diagonal)
                    if diagonal:
                        last = nc.tensor.matmul(out[:, col:col + P], identr[:], T["mask_kq"][:], start=False, stop=True)
                last.then_inc(scored, 1)

            def weigh(b, n, g, u):
                c, parts = UNITS[u]
                head, s = b * HEADS + 4 * g + n, (n * NU + u) % RING
                pe.wait_ge(lo_pool if ON_POOL[u] else lo_dve, lo_count(head, u, ON_POOL[u]))
                if parts[0][0] == 0 and (n > 0 or c == 0):
                    pe.wait_ge(o_free[c], head)
                for kt, q0, w, col in parts:
                    for part in range(2):
                        ins = nc.tensor.matmul(obank[0:3 * HD, c, q0 - c * HALF:q0 - c * HALF + w], vs[:, kt, :],
                                               prs[s][:, part, col:col + w], start=(kt == 0 and part == 0),
                                               stop=(kt == UNITS[(C0_UNITS, NU)[c] - 1][1][-1][0] and part == 1))
                ins.then_inc(pv_done, 1)

            def weigh_late(b, n, g, u):
                if u >= LAG:
                    weigh(b, n, g, u - LAG)
                elif n > 0:
                    weigh(b, n - 1, g, u - LAG + NU)

            def step(b, n, g, has_q, has_max):
                if has_q:
                    project_q(b, g, g + 1, SIDE_LOOP)
                for u in range(NU):
                    score(b, n, g, u)
                    weigh_late(b, n, g, u)
                    if has_max:
                        for i, at in enumerate(SLOT_UNITS):
                            if at == u:
                                max_slot(b, n + 2, g, i)
                if n == 15:
                    for u in range(NU - LAG, NU):
                        weigh(b, n, g, u)
                if has_max:
                    max_slot(b, n + 2, g, NS - 1)

            with pe.Fori(0, B) as b:
                for t in range(TT):
                    pe.wait_ge(xn_ready, b * TT + t + 1)
                    if t == 4:
                        pe.wait_ge(h_ready, b * 2 * KT + KT)
                    for k in range(KT):
                        last = nc.tensor.transpose(scores(k)[:, (t % 4) * P:(t % 4 + 1) * P],
                                                   xn[:, t % 2, k * P:(k + 1) * P], ident[:])
                    last.then_inc(xt_done, 1)
                for h in range(2):
                    pe.wait_ge(ht_ready, b * 2 * KT + (h + 1) * KT)
                    r = side_bank(b, SIDE_KV + h)
                    product(side[:, r, :], lambda p, k: kvw[:, p, k, :],
                            lambda p, k: ht[:, p, k, h * HALF:(h + 1) * HALF], KT).then_inc(side_full[r], 1)
                project_q(b, 0, 0, SIDE_Q0)
                for h in range(2):
                    side_taken(pe, b, SIDE_KV + h)
                pe.wait_ge(o_free[0], b * HEADS)
                pe.wait_ge(kst_ready, b + 1)
                for i in range(NS):
                    max_slot(b, 0, 0, i)
                for t in range(TT):
                    last = nc.tensor.transpose(obank[:, 0, t * HD:(t + 1) * HD], kv[96:P, t * P:(t + 1) * P], ident[96:P, 96:P])
                last.then_inc(vt_done, 1)
                for i in range(NS):
                    max_slot(b, 1, 0, i)
                pe.wait_ge(vs_lo, b + 1)
                step(b, 0, 0, False, True)
                with pe.Fori(0, 3) as g:
                    for n in range(1, 5):
                        step(b, n, g, n == 1, True)
                for n in range(13, 16):
                    step(b, n, 0, False, n == 13)
                for t in range(TT):
                    if t == 0:
                        pe.wait_ge(group_normed, (b + 1) * GROUPS)
                    r = side_bank(b, SIDE_OUT + t)
                    product(side[:, r, :], lambda p, k: ot[:, p, k, t * P:(t + 1) * P],
                            lambda p, k: ow[:, p, k, :], KT, last=False)
                    nc.tensor.matmul(side[:, r, :], T["ones"][:], T["ob"][:], start=False, stop=True).then_inc(side_full[r], 1)


def ffn_setup(nc, io, B, sem, sb, bank, W):
    had = sb("hadamard", [P, P])
    su = sb("signs", [P, KT + FT])
    but = sb("butterfly", [P, KT, HALF])
    wm = sb("wmod_gb", [P, KT, D])
    ct, cs, cbc = sb("c_t2", [P, KT, B]), sb("c_silu2", [P, KT, B]), sb("c_bcast2", [P, KT, B, P])
    wsd = sb("wscale_down", [P, D])
    fl = sb("floor_tmp2", [P, 3, D])
    CH = FF // HALF
    small_in, wm_in = sem("ffn_small_in"), sem("wmod_gb_in")
    ug_in, d_in = [sem(f"ug_in{n}") for n in range(2 * CH)], sem("down_in")
    silu_done, cbc_ready, g_done, g_free = sem("silu_c_done2"), sem("cbc_ready2"), sem("gb_done"), sem("gb_free")
    su_ready, crossed, folded, evacuated, dve_step = sem("su_ready"), sem("crossed"), sem("folded"), sem("evacuated"), sem("ffn_setup_step")
    down, upgate = W["d"], W["ug"]

    def chunk(c):
        return upgate[:, :, c // CH, (c % CH) * HALF:(c % CH + 1) * HALF]

    tiles = [(chunk(c)[:, k, :], su_at) for c in range(2 * CH) for k in range(KT) for su_at in (k,)]
    tiles += [(down[:, f, :], KT + f) for f in range(FT)]

    with nc.Block() as block:
        @block.sync
        def _(sp):
            sp.dma_start(had[:], io["had"]).then_inc(small_in, 16)
            sp.dma_start(su[:, 0:KT], io["su_ug"]).then_inc(small_in, 16)
            sp.dma_start(su[:, KT:], io["su_dp"]).then_inc(small_in, 16)
            sp.dma_start(W["sug"][:], io["ws_ug"]).then_inc(small_in, 16)
            sp.dma_start(ct[:], io["cT"]).then_inc(small_in, 16)
            sp.dma_start(wsd[:], io["ws_dp"].to_broadcast([P, D])).then_inc(small_in, 16)
            for c in range(2 * CH):
                src = io["w_up"] if c < CH else io["w_gate"]
                sp.dma_start(chunk(c), src.rearrange("(k p) n -> p k n", p=P)[:, :, (c % CH) * HALF:(c % CH + 1) * HALF]).then_inc(ug_in[c], 16)
            sp.dma_start(down[:], io["w_down"].rearrange("(f p) n -> p f n", p=P)).then_inc(d_in, 16)
            sp.dma_start(wm[:], io["wmod"].rearrange("(k p) n -> p k n", p=P)[:, :, 5 * D:6 * D]).then_inc(wm_in, 16)

        @block.scalar
        def _(act):
            act.wait_ge(small_in, 96)
            nc.scalar.activation(cs[:], ct[:], ACT.Silu).then_inc(silu_done, 1)
            act.wait_ge(su_ready, 1)
            for n, (at, s) in enumerate(tiles):
                act.wait_ge(folded, n + 1)
                nc.scalar.activation(at, bank[n % 4 // 2][:, n % 2, :], ACT.Copy, scale=su[:, s:s + 1]).then_inc(evacuated, 1)

        @block.tensor
        def _(pe):
            pe.wait_ge(small_in, 96)
            for n, (at, s) in enumerate(tiles):
                pe.wait_ge(crossed, n // KT + 1 if n < 2 * CH * KT else 2 * CH + 4)
                if n >= 4:
                    pe.wait_ge(evacuated, n - 3)
                nc.tensor.matmul(bank[n % 4 // 2][:, n % 2, :], had[:], at, start=True, stop=True).then_inc(folded, 1)
            pe.wait_ge(cbc_ready, 1)
            pe.wait_ge(wm_in, 16)
            for b in range(B):
                if b >= 2:
                    pe.wait_ge(g_free, b - 1)
                for k in range(KT):
                    last = nc.tensor.matmul(bank[2][:, b % 2, :], cbc[:, k, b, :], wm[:, k, :], start=(k == 0), stop=(k == KT - 1))
                last.then_inc(g_done, 1)

        @block.vector
        def _(dve):
            chain = Chain(dve, dve_step)
            dve.wait_ge(small_in, 96)
            nc.vector.tensor_scalar(su[:, 0:KT], su[:, 0:KT], float(D) ** -0.5, None, ALU.mult)
            nc.vector.tensor_scalar(su[:, KT:], su[:, KT:], float(FF) ** -0.5, None, ALU.mult).then_inc(su_ready, 1)
            dve.wait_ge(silu_done, 1)
            nc.vector.tensor_copy(cbc[:], cs[:].unsqueeze(3).to_broadcast([P, KT, B, P])).then_inc(cbc_ready, 1)
            for c in range(2 * CH):
                w = chunk(c)
                dve.wait_ge(ug_in[c], 16)
                pairs, to = w.rearrange("p (a two) n -> p a two n", two=2), but[:].rearrange("p (a two) n -> p a two n", two=2)
                nc.vector.tensor_tensor(to[:, :, 0], pairs[:, :, 0], pairs[:, :, 1], ALU.add)
                chain.link(nc.vector.tensor_tensor(to[:, :, 1], pairs[:, :, 0], pairs[:, :, 1], ALU.subtract))
                nc.vector.tensor_tensor(w[:, 0:2], but[:, 0:2], but[:, 2:4], ALU.add)
                last = nc.vector.tensor_tensor(w[:, 2:4], but[:, 0:2], but[:, 2:4], ALU.subtract)
                last.then_inc(crossed, 1)
                dve.wait_ge(crossed, c + 1)
            dve.wait_ge(d_in, 16)
            for c in range(4):
                w = down[:, :, c * P:(c + 1) * P]
                t = but[:].rearrange("p k n -> p (k n)").rearrange("p (f n) -> p f n", n=P)
                for stage, (a, z) in enumerate(((w, t), (t, w), (w, t), (t, w))):
                    h = 2 ** stage
                    i = a.rearrange("p (a two h) n -> p a two h n", two=2, h=h)
                    o = z.rearrange("p (a two h) n -> p a two h n", two=2, h=h)
                    nc.vector.tensor_tensor(o[:, :, 0], i[:, :, 0], i[:, :, 1], ALU.add)
                    last = nc.vector.tensor_tensor(o[:, :, 1], i[:, :, 0], i[:, :, 1], ALU.subtract)
                    if stage < 3:
                        chain.link(last)
                last.then_inc(crossed, 1)
                dve.wait_ge(crossed, 2 * CH + c + 1)
            for b in range(B):
                dve.wait_ge(g_done, b + 1)
                floored(nc, chain, W["gbw"][:, b, :], bank[2][:, b % 2, :], fl, g_free, b + 1)
                nc.vector.tensor_tensor(W["gbw"][:, b, :], W["gbw"][:, b, :], wsd[:], ALU.mult)


def ffn_phase(nc, io, B, S, sem, sb, bank, ident, mod, eps, W, x1_dram):
    NT = HALF // P
    up, gate, acc = bank[0], bank[1], (bank[2], bank[3])
    modb = sb("mod_batch2", [P, 2, KT, 1])
    x1 = sb("x1_in", [P, 2, NT, D])
    xn = sb("x1_normed", [P, NT, D])
    hs = sb("h2_t", [P, KT, HALF])
    ht = sb("h2_t_split", [P, 2, KT, HALF], F32R)
    wr = [[sb(f"w_ring{n}_{p}", [P, KT, 2, P], F32R) for p in range(2)] for n in range(2)]
    dr = [[sb(f"d_ring{n}_{p}", [P, D], F32R) for p in range(2)] for n in range(2)]
    sg = sb("silu_gate", [P, 2, HALF])
    y = sb("y", [P, HALF])
    ys = [sb(f"y_split{n}", [P, 2, HALF], F32R) for n in range(2)]
    out_sb, tmp = sb("out_sb", [P, 2, D]), sb("out_tmp", [P, 2, D])
    st6, mv, rs = sb("ln2_stats", [P, NT, 6]), sb("ln2_mean_var", [P, NT, 2]), sb("ln2_rstd", [P, 2, NT])

    x1_in = [sem("x1_in0"), sem("x1_in1")]
    stats_ready, sd_ready, xn_ready, xt_done, h_ready, ht_ready = (
        sem(n) for n in ("stats2_ready", "sd2_ready", "xn2_ready", "xt2_done", "h2_ready", "ht2_ready"))
    ug_cast, d_cast, ug_ready, d_ready = sem("ug_cast"), sem("d_cast"), sem("ug_ready"), sem("d_ready")
    ug_done, silu_done, y_mul, y_ready, d_done = sem("ug_done"), sem("silu_done"), sem("y_mul"), sem("y_ready"), sem("d_done")
    out_ready, stored, dve_step = sem("out_ready"), [sem("stored0"), sem("stored1")], sem("ffn_dve_step")
    PAIRS = FT // 2

    def at_tile(n):
        return n if isinstance(n, int) else bass.ds(n, 1)

    def pairs(engine, body, chain=None, per_pass=0):
        body(0, True, False)
        with engine.Fori(1, PAIRS - 1) as p:
            if chain:
                inner = chain.loop(p - 1, per_pass)
            body(p, False, False)
            if chain:
                chain.end(inner, PAIRS - 2)
        body(PAIRS - 1, False, True)

    def h_bank(k):
        return bank[k % 2][:, k // 2, :]

    def blocks(engine, block_of, chain=None, per_batch=0):
        with engine.Fori(0, B - 1) as b:
            if chain:
                outer = chain.loop(b, per_batch)
            block_of(b, 0, True)
            block_of(b, 1, True)
            if chain:
                chain.end(outer, B - 1)
        block_of(B - 1, 0, True)
        block_of(B - 1, 1, False)

    with nc.Block() as block:
        @block.gpsimd
        def _(pool):
            with pool.Fori(0, B) as b:
                for h in range(2):
                    pool.wait_ge(out_ready, (2 * b + h + 1) * NT)
                    pool.dma_start(x1[:, h], x1_dram[b, NT * h:NT * (h + 1)].rearrange("t p n -> p t n")).then_inc(x1_in[h], 16)

        @block.sync
        def _(sp):
            with sp.Fori(0, B) as b:
                for t in range(2 * NT):
                    sp.wait_ge(out_ready, (b + 1) * 2 * NT + t + 1)
                    sp.dma_start(io["out"][b, t], out_sb[:, t % 2, :]).then_inc(stored[t % 2], 16)
            for n in range(2):
                sp.wait_ge(stored[n], 16 * B * NT)

        @block.scalar
        def _(act):
            def deviations(b, blk):
                nc.scalar.activation(modb[:], mod[:, 2:4, :, at_tile(b)], ACT.Copy)
                act.wait_ge(stats_ready, blk + 1)
                nc.scalar.activation(rs[:, 0, :], mv[:, :, 1], ACT.Sqrt, bias=eps[:]).then_inc(sd_ready, 1)

            def modulate(blk, ks):
                for k in ks:
                    act.wait_ge(xt_done, blk * KT + k + 1)
                    nc.scalar.activation(hs[:, k, :], h_bank(k), ACT.Identity,
                                         bias=modb[:, 0, k, :], scale=modb[:, 1, k, :]).then_inc(h_ready, 1)

            def cast_ug(f, s, at):
                act.wait_ge(ug_done, f - 1)
                nc.scalar.activation(wr[s][0][:], W["ug"][:, :, :, bass.ds(at * P, P)], ACT.Copy).then_inc(ug_cast, 1)

            nc.scalar.activation(wr[0][0][:], W["ug"][:, :, :, 0:P], ACT.Copy).then_inc(ug_cast, 1)
            nc.scalar.activation(dr[0][0][:], W["d"][:, 0, :], ACT.Copy).then_inc(d_cast, 1)
            deviations(0, 0)
            modulate(0, range(KT))

            def block_of(b, h, has_next):
                blk = 2 * b + h

                def body(p, first, last):
                    for e in range(2):
                        f, s = blk * FT + 2 * p + e, e
                        ends = last and e == 1
                        at = 0 if ends else 2 * p + e + 1
                        if has_next or not ends:
                            cast_ug(f + 1, 1 - s, at)
                        act.wait_ge(ug_done, f + 1)
                        nc.scalar.activation(sg[:, s, :], gate[:, s, :], ACT.Silu,
                                             scale=W["sug"][:, 1, bass.ds(2 * p + e, 1)]).then_inc(silu_done, 1)
                        if has_next and ends:
                            modulate(blk + 1, (0, 1))
                        if has_next or not ends:
                            act.wait_ge(d_done, f)
                            nc.scalar.activation(dr[1 - s][0][:], W["d"][:, at_tile(at), :], ACT.Copy).then_inc(d_cast, 1)
                    if has_next and first:
                        deviations(b + h, blk + 1)
                    if has_next and last:
                        modulate(blk + 1, (2, 3))
                pairs(act, body)
            blocks(act, block_of)

        @block.vector
        def _(dve):
            chain = Chain(dve, dve_step)
            nc.vector.memset(tmp[:, 0, :], 0.0).then_inc(out_ready, 2 * NT)

            def statistics(batch, half, blk):
                dve.wait_ge(x1_in[half], 16 * (batch + 1))
                for t in range(NT):
                    last = nc.vector.bn_stats(st6[:, t, :], x1[:, half, t, :])
                chain.link(last)
                nc.vector.memset(eps[:], EPS)
                for t in range(NT):
                    last = nc.vector.bn_aggr(mv[:, t, :], st6[:, t, :])
                last.then_inc(stats_ready, 1)

            def normalise(half, blk):
                dve.wait_ge(sd_ready, blk + 1)
                chain.link(nc.vector.reciprocal(rs[:, 1, :], rs[:, 0, :]))
                for t in range(NT):
                    last = nc.vector.tensor_scalar(xn[:, t, :], x1[:, half, t, :], mv[:, t, 0:1], rs[:, 1, t:t + 1],
                                                   ALU.subtract, ALU.mult)
                last.then_inc(xn_ready, 1)

            def split_h(blk, ks):
                for k in ks:
                    dve.wait_ge(h_ready, blk * KT + k + 1)
                    chain.link(nc.vector.tensor_copy(ht[:, 0, k, :], hs[:, k, :]))
                    nc.vector.tensor_tensor(ht[:, 1, k, :], hs[:, k, :], ht[:, 0, k, :].bitcast(F32),
                                            ALU.subtract).then_inc(ht_ready, 1)

            def split_ug(f, s, at):
                dve.wait_ge(ug_cast, f + 1)
                nc.vector.tensor_tensor(wr[s][1][:], W["ug"][:, :, :, bass.ds(at * P, P)], wr[s][0][:].bitcast(F32),
                                        ALU.subtract).then_inc(ug_ready, 1)

            def split_d(f, s, at):
                dve.wait_ge(d_cast, f + 1)
                nc.vector.tensor_tensor(dr[s][1][:], W["d"][:, at_tile(at), :], dr[s][0][:].bitcast(F32), ALU.subtract).then_inc(d_ready, 1)

            statistics(0, 0, 0)
            normalise(0, 0)
            split_ug(0, 0, 0)
            split_d(0, 0, 0)
            split_h(0, range(KT))

            def block_of(b, h, has_next):
                blk = 2 * b + h

                def body(p, first, last):
                    for e in range(2):
                        f, s = blk * FT + 2 * p + e, e
                        ends = last and e == 1
                        at = 0 if ends else 2 * p + e + 1
                        if has_next or not ends:
                            split_ug(f + 1, 1 - s, at)
                        if not (isinstance(b, int) and b == 0 and h == 0 and first and e == 0):
                            dve.wait_ge(y_ready, f)
                        dve.wait_ge(silu_done, f + 1)
                        ins = nc.vector.scalar_tensor_tensor(out=y[:], in0=up[:, s, :], scalar=W["sug"][:, 0, bass.ds(2 * p + e, 1)],
                                                             in1=sg[:, s, :], op0=ALU.mult, op1=ALU.mult)
                        ins.then_inc(y_mul, 1)
                        dve.wait_ge(y_mul, f + 1)
                        if not first:
                            dve.wait_ge(d_done, f - 1)
                        chain.link(nc.vector.tensor_copy(ys[s][:, 0, :], y[:]))
                        nc.vector.tensor_tensor(ys[s][:, 1, :], y[:], ys[s][:, 0, :].bitcast(F32), ALU.subtract).then_inc(y_ready, 1)
                        if has_next and ends:
                            split_h(blk + 1, (0, 1))
                        if has_next or not ends:
                            split_d(f + 1, 1 - s, at)
                        if has_next and last and e == 0:
                            normalise(1 - h, blk + 1)
                    if has_next and first:
                        statistics(b + h, 1 - h, blk + 1)
                    if has_next and last:
                        split_h(blk + 1, (2, 3))
                pairs(dve, body, chain, 2)
                dve.wait_ge(d_done, (blk + 1) * FT)
                for t in range(NT):
                    chain.link(nc.vector.tensor_tensor(tmp[:, t % 2, :], acc[t // 2][:, t % 2, :], W["gbw"][:, b, :], ALU.mult))
                    dve.wait_ge(stored[t % 2], 16 * (blk * NT // 2 + t // 2))
                    ins = nc.vector.tensor_tensor(out_sb[:, t % 2, :], tmp[:, t % 2, :], x1[:, h, t, :], ALU.add)
                    ins.then_inc(out_ready, 1)
            blocks(dve, block_of, chain, 2 * (2 + KT + FT + NT))

        @block.tensor
        def _(pe):
            def transposes(blk, ks):
                pe.wait_ge(xn_ready, blk + 1)
                for k in ks:
                    for t in range(NT):
                        last = nc.tensor.transpose(h_bank(k)[:, t * P:(t + 1) * P], xn[:, t, k * P:(k + 1) * P], ident[:])
                    last.then_inc(xt_done, 1)

            def up_gate(f, s):
                pe.wait_ge(ug_ready, f + 1)
                for side in range(2):
                    for k in range(KT):
                        for a, m in ((0, 0), (0, 1), (1, 0)):
                            last = nc.tensor.matmul(bank[side][:, s, :], wr[s][a][:, k, side, :], ht[:, m, k, :],
                                                    start=(k == 0 and a + m == 0), stop=(k == KT - 1 and a == 1))
                last.then_inc(ug_done, 1)

            def down(f, s, first, last_one):
                pe.wait_ge(y_ready, f + 1)
                pe.wait_ge(d_ready, f + 1)
                for t in range(NT):
                    for a, m in ((0, 0), (0, 1), (1, 0)):
                        last = nc.tensor.matmul(acc[t // 2][:, t % 2, :], ys[s][:, a, t * P:(t + 1) * P], dr[s][m][:],
                                                start=(first and a + m == 0), stop=(last_one and a == 1))
                last.then_inc(d_done, 1)

            def block_of(b, h, has_next):
                blk = 2 * b + h
                pe.wait_ge(ht_ready, (blk + 1) * KT)

                def body(p, first, last):
                    f = blk * FT + 2 * p
                    for e in range(2):
                        if not first:
                            pe.wait_ge(y_mul, f + e - 1)
                        up_gate(f + e, e)
                        if has_next and last and e:
                            pe.wait_ge(y_mul, f + 1)
                            transposes(blk + 1, (0, 1))
                        if e:
                            if first:
                                pe.wait_ge(out_ready, (blk + 2) * NT)
                            down(f, 0, first, False)
                        elif not first:
                            down(f - 1, 1, False, False)
                    if has_next and last:
                        pe.wait_ge(y_mul, f + 2)
                        transposes(blk + 1, (2, 3))
                    if last:
                        down(f + 1, 1, False, True)
                pairs(pe, body)

            transposes(0, range(KT))
            blocks(pe, block_of)


def hadamard(n):
    import numpy as np
    return np.array([[1.0 - 2.0 * (bin(i & j).count("1") % 2) for j in range(n)] for i in range(n)], np.float32)


def kernel(**inputs):
    import numpy as np
    import concourse.bacc as bacc
    from concourse.bass_utils import run_bass_kernel_spmd

    a = {name.removeprefix("L0_"): np.asarray(v) for name, v in inputs.items()}
    x = a["attn_hidden_states"]
    B, S, _ = x.shape

    def lay(v):
        return np.ascontiguousarray(v)

    def columns(v):
        return lay(v.reshape(-1, P).T)

    arrays = dict(
        x=lay(x.reshape(B, S // P, P, D)),
        cT=lay(a["c"].T.reshape(KT, P, B).transpose(1, 0, 2)),
        wmod=lay(a["wmod"]),
        qwT=lay(a["attn_q_w"].T), kwT=lay(a["attn_k_w"].T), vwT=lay(a["attn_v_w"].T), owT=lay(a["attn_o_w"].T),
        qb=lay(np.concatenate([a["attn_q_b"], a["attn_q_b"][:P]]).reshape(GROUPS + 1, P, 1)), kb=lay(a["attn_k_b"].reshape(HD, 1)), vb=lay(a["attn_v_b"].reshape(HD, 1)),
        ob=lay(a["attn_o_b"].reshape(1, D)),
        su_ug=columns(a["ffn_SU_ug"]), su_dp=columns(a["ffn_SU_dp"]),
        ws_ug=lay(a["ffn_Wscale_ug"].reshape(2, FT, P).transpose(2, 0, 1)), ws_dp=lay(a["ffn_Wscale_dp"].reshape(1, D)),
        w_up=lay(a["ffn_W_up"].T), w_gate=lay(a["ffn_W_gate"].T), w_down=lay(a["ffn_W_down"].T),
        had=hadamard(P),
    )
    nc = bacc.Bacc("TRN2", target_bir_lowering=False, num_devices=1)
    io = {k: nc.dram_tensor(f"in_{k}", v.shape, mybir.dt.from_np(v.dtype), kind="ExternalInput").ap() for k, v in arrays.items()}
    io["out"] = nc.dram_tensor("out", (B, S // P, P, D), F32, kind="ExternalOutput").ap()
    program(nc, io, B, S)
    r = run_bass_kernel_spmd(nc, [{f"in_{k}": v for k, v in arrays.items()}], core_ids=[0])
    return r.results[0]["out"].reshape(B, S, D)
```

```python
import concourse.bass as bass
from concourse import mybir
from contextlib import ExitStack

F32 = mybir.dt.float32
F32R = mybir.dt.float32r
ALU = mybir.AluOpType
ACT = mybir.ActivationFunctionType
AX = mybir.AxisListType

P = 128
D = 512
KT = D // P
HEADS = 16
HD = D // HEADS
GROUPS = KT
FF = 2048
FT = FF // P
HALF = 512
SCALE = HD ** -0.5
EPS = 1e-5
BIG = 2.0 ** 100

UNITS = [
    (0, [(0, 0, 512, 0)]), (0, [(1, 128, 384, 0), (3, 384, 128, 384)]), (0, [(2, 256, 256, 0)]),
    (1, [(0, 512, 512, 0)]), (1, [(1, 512, 512, 0)]), (1, [(2, 512, 512, 0)]), (1, [(3, 512, 512, 0)]),
    (1, [(4, 512, 512, 0)]), (1, [(5, 640, 384, 0), (7, 896, 128, 384)]), (1, [(6, 768, 256, 0)]),
]
NU = len(UNITS)
C0_UNITS = sum(c == 0 for c, _ in UNITS)
RING = 4
LAG = 3
ON_POOL = [u % 5 in (0, 2, 4) for u in range(NU)]
SLOTS = [
    [(3, 0, 512, 0)], [(4, 0, 512, 0)], [(5, 0, 512, 0)], [(6, 0, 512, 0)], [(7, 0, 512, 0)], [(7, 512, 512, 0)],
    [(6, 512, 384, 0), (0, 0, 128, 384)], [(2, 0, 384, 0), (4, 512, 128, 384)], [(5, 512, 256, 0), (1, 0, 256, 256)],
]
SLOT_UNITS = [0, 0, 1, 2, 3, 4, 5, 6, 6]
NS = len(SLOTS) + 1

FIRST_STEPS, LOOP_STEPS, LAST_STEPS, PASSES = (0, 1), (2, 3, 4, 5), (10, 11, 12, 13, 14, 15), 2
Q_STEPS, NORM_STEPS = (1, 5), (5, 13)
NORM_PIECES = {1: (0,), 2: (1, 3), 3: (4, 2), 4: (5,)}
LAST_MAX_STEP = HEADS - 3

SIDE_STEP, SIDE_AT = {}, 0
for _n in FIRST_STEPS + LOOP_STEPS:
    SIDE_STEP[_n] = SIDE_AT
    SIDE_AT += NS + 2 * (_n in Q_STEPS)
SIDE_PER_PASS = SIDE_AT - SIDE_STEP[LOOP_STEPS[0]]
SIDE_AT += (PASSES - 1) * SIDE_PER_PASS
for _n in LAST_STEPS:
    SIDE_STEP[_n] = SIDE_AT
    SIDE_AT += NS * (_n <= LAST_MAX_STEP)
SIDE_EDGE = SIDE_AT


def edge_order(has_prev, has_next):
    order = []
    if has_next:
        order += [("kv", 0), ("q", 0), ("kv", 1), ("q", 1)]
    slots = [("max", 0, i) for i in range(NS)] + [("max", 1, i) for i in range(NS)]
    for t, take in enumerate((0, 2, 3, 2, 2, 4, 3, 4)):
        if has_prev:
            order.append(("out", t))
        if has_next:
            order += slots[:take]
            slots = slots[take:]
    return order


SIDE_FIRST = -len(edge_order(False, True))
SIDE_ALL = SIDE_EDGE + len(edge_order(True, True))


class Chain:

    def __init__(self, engine, sem):
        self.engine, self.sem, self.base, self.n = engine, sem, 0, 0

    def link(self, instruction):
        self.n += 1
        instruction.then_inc(self.sem, 1)
        self.engine.wait_ge(self.sem, self.base + self.n)

    def loop(self, register, per_pass):
        outer = (self.base, self.n, per_pass)
        self.base, self.n = self.base + self.n + register * per_pass, 0
        return outer

    def end(self, outer, passes):
        assert self.n == outer[2], (self.n, outer)
        self.base, self.n = outer[0], outer[1] + passes * outer[2]


def program(nc, io, B, S):
    TT = S // P
    assert S == 2 * HALF and TT == 8
    x1_dram = nc.dram_tensor("x1_dram", (B, TT, P, D), F32).ap()
    gains_dram = nc.dram_tensor("gains_dram", (2, B, D), F32).ap()
    inverse_dram = nc.dram_tensor("inverse_sums_dram", (4, S), F32).ap()
    qw_dram = nc.dram_tensor("qw_split_dram", (GROUPS + 1, P, 2, KT, P), F32).ap()
    ctx = ExitStack()
    with ctx:
        def sem(name):
            return ctx.enter_context(nc.semaphore(name))

        def sb(stack, name, shape, dt=F32):
            return stack.enter_context(nc.sbuf_tensor(name, shape, dt))

        bank = [ctx.enter_context(nc.psum_tensor(f"bank{n}", [P, 2, HALF], F32)) for n in range(4)]
        ident = sb(ctx, "ident", [P, P])
        mod = sb(ctx, "mod", [P, 4, KT, B])
        eps = sb(ctx, "eps", [P, 1])
        with ExitStack() as attention:
            T = dict(
                ow=sb(attention, "ow_split", [P, 2, KT, D], F32R),
                kvw=sb(attention, "kvw_split", [P, 2, KT, P], F32R),
                identr=sb(attention, "identr", [P, P], F32R),
                mask_kq=sb(attention, "mask_kq", [P, P], F32R),
                mask_qk=sb(attention, "mask_qk", [P, P], F32R),
                kvb=sb(attention, "kvb", [P, 1]),
                ga=sb(attention, "ga", [P, B, D]), ob=sb(attention, "ob_split", [2, D], F32R), ones=sb(attention, "ones2", [2, P], F32R),
                x=sb(attention, "x", [P, TT, D]), x_in=[sem(f"x_in{t}") for t in range(TT)],
                st6=sb(attention, "ln_stats", [P, TT, 6]), mv=sb(attention, "ln_mean_var", [P, TT, 2]),
                rs=sb(attention, "ln_rstd", [P, 2, TT]),
                stats_ready=sem("stats_ready"), sd_ready=sem("sd_ready"), xn_ready=sem("xn_ready"),
                kst=sb(attention, "k_stack", [98, S], F32R),
                vs=sb(attention, "v_split_ones", [P, TT, 3 * HD], F32R),
            )
            with ExitStack() as temps:
                attention_setup(nc, io, B, sem, lambda *a: sb(temps, *a), bank, ident, mod, eps, T, qw_dram, gains_dram)
            attention_phase(nc, io, B, S, sem, lambda *a: sb(attention, *a), bank, ident, mod, eps, T, qw_dram, inverse_dram, x1_dram)
        with ExitStack() as ffn:
            W = dict(
                ug=sb(ffn, "w_upgate", [P, KT, 2, FF]), d=sb(ffn, "w_down", [P, FT, D]),
                sug=sb(ffn, "scale_upgate", [P, 2, FT]), gbw=sb(ffn, "gbw", [P, B, D]),
                x1=sb(ffn, "x1_in", [P, 2, HALF // P, D]), x1_in=[sem("x1_in0"), sem("x1_in1")],
            )
            with ExitStack() as temps:
                ffn_setup(nc, io, B, sem, lambda *a: sb(temps, *a), bank, W, gains_dram, x1_dram)
            ffn_phase(nc, io, B, S, sem, lambda *a: sb(ffn, *a), bank, ident, mod, eps, W, x1_dram)


def layer_norm_statistics(nc, dve, chain, T, eps, b, t):
    dve.wait_ge(T["x_in"][t], 16 * (b + 1))
    tiles = len(T["x_in"])
    last = nc.vector.bn_stats(T["st6"][:, t, :], T["x"][:, t, :])
    if t == tiles - 1:
        chain.link(last)
        nc.vector.memset(eps[:], EPS)
        for n in range(tiles):
            last = nc.vector.bn_aggr(T["mv"][:, n, :], T["st6"][:, n, :])
        last.then_inc(T["stats_ready"], 1)


def layer_norm_tile(nc, dve, chain, T, b, t):
    x, mv, rs = T["x"], T["mv"], T["rs"]
    if t == 0:
        dve.wait_ge(T["sd_ready"], b + 1)
        chain.link(nc.vector.reciprocal(rs[:, 1, :], rs[:, 0, :]))
    nc.vector.tensor_scalar(x[:, t, :], x[:, t, :], mv[:, t, 0:1], rs[:, 1, t:t + 1],
                            ALU.subtract, ALU.mult).then_inc(T["xn_ready"], 1)


def layer_norm_deviations(nc, act, T, eps, b):
    act.wait_ge(T["stats_ready"], b + 1)
    nc.scalar.activation(T["rs"][:, 0, :], T["mv"][:, :, 1], ACT.Sqrt, bias=eps[:]).then_inc(T["sd_ready"], 1)


def attention_setup(nc, io, B, sem, sb, bank, ident, mod, eps, T, qw_dram, gains_dram):
    wm = sb("wmod_sb", [P, 6, KT, D])
    ct = sb("c_t", [P, KT, B])
    cs = sb("c_silu", [P, KT, B])
    qraw = sb("qw_raw", [P, KT, D])
    qsp = sb("qw_split", [P, 2, KT, D], F32R)
    oraw = sb("ow_raw", [P, KT, D])
    kvraw = sb("kvw_raw", [P, KT, P])
    obr, obs, ones = sb("ob_raw", [1, D]), sb("ob_hi_lo", [1, 2, D], F32R), sb("ones", [2, P])
    mk = sb("masks", [P, 2, P])
    gains, fl = sb("gains", [B, 2, D]), sb("floor_tmp", [B, 3, 2 * D])
    c_in, wm_in, w_in, bias_in = sem("c_in"), [sem(f"wmod_in{n}") for n in range(6)], sem("attn_w_in"), sem("attn_bias_in")
    const_step, const_ready = sem("const_step"), sem("const_ready")
    silu_done, mod_done, g_done = sem("silu_c_done"), sem("mod_done"), sem("gains_done")
    g_ready, g_out, ga_in = sem("gains_ready"), sem("gains_out"), sem("ga_in")
    dve_step, split_ready, qw_out, ob_split = sem("setup_dve_step"), sem("qw_split_ready"), sem("qw_out"), sem("ob_split")

    with nc.Block() as block:
        @block.sync
        def _(sp):
            sp.dma_start(ct[:], io["cT"]).then_inc(c_in, 16)
            wmv = io["wmod"].rearrange("(k p) (m n) -> m p k n", p=P, n=D)
            for m in (2, 5):
                sp.dma_start(wm[:, m, :, :], wmv[m]).then_inc(wm_in[m], 16)
            for t in range(len(T["x_in"])):
                sp.dma_start(T["x"][:, t, :], io["x"][0, t]).then_inc(T["x_in"][t], 16)
            for m in (0, 1, 3, 4):
                sp.dma_start(wm[:, m, :, :], wmv[m]).then_inc(wm_in[m], 16)
            sp.dma_start(qraw[:], io["qwT"].rearrange("(k p) n -> p k n", p=P)).then_inc(w_in, 16)
            sp.dma_start(oraw[:], io["owT"].rearrange("(k p) n -> p k n", p=P)).then_inc(w_in, 16)
            for r in range(3):
                sp.dma_start(kvraw[:, :, r * HD:(r + 1) * HD], io["kwT"].rearrange("(k p) n -> p k n", p=P)).then_inc(w_in, 16)
                sp.dma_start(T["kvb"][r * HD:(r + 1) * HD, :], io["kb"]).then_inc(bias_in, 16)
            sp.dma_start(kvraw[:, :, 96:P], io["vwT"].rearrange("(k p) n -> p k n", p=P)).then_inc(w_in, 16)
            sp.dma_start(T["kvb"][96:P, :], io["vb"]).then_inc(bias_in, 16)
            sp.dma_start(obr[:], io["ob"]).then_inc(bias_in, 16)
            sp.wait_ge(g_ready, 1)
            sp.dma_start(gains_dram.rearrange("g b n -> b g n"), gains[:]).then_inc(g_out, 16)
            sp.wait_ge(g_out, 16)
            sp.dma_start(T["ga"][:], gains_dram[0:1].to_broadcast([P, B, D])).then_inc(ga_in, 16)
            sp.wait_ge(split_ready, 1)
            for g in range(GROUPS + 1):
                at = g % GROUPS * P
                sp.dma_start(qw_dram[g], qsp[:, :, :, at:at + P].bitcast(F32)).then_inc(qw_out, 16)
            sp.wait_ge(qw_out, 16 * (GROUPS + 1))
            sp.wait_ge(ob_split, 1)
            for part in range(2):
                sp.dma_start(T["ob"][part:part + 1, :].bitcast(F32), obs[:, part, :].bitcast(F32)).then_inc(qw_out, 16)
            sp.wait_ge(qw_out, 16 * (GROUPS + 3))
            sp.wait_ge(ga_in, 16)

        @block.gpsimd
        def _(pool):
            nc.gpsimd.memset(ident[:], 0.0).then_inc(const_step, 1)
            nc.gpsimd.memset(mk[:], 0.0).then_inc(const_step, 1)
            pool.wait_ge(const_step, 2)
            nc.gpsimd.affine_select(out=ident[:], in_=ident[:], compare_op=ALU.not_equal, fill=1.0, base=0,
                                    pattern=[[-1, P]], channel_multiplier=1).then_inc(const_ready, 1)
            nc.gpsimd.affine_select(out=mk[:, 0, :], in_=mk[:, 0, :], compare_op=ALU.is_ge, fill=-BIG, base=0,
                                    pattern=[[1, P]], channel_multiplier=-1).then_inc(const_ready, 1)
            nc.gpsimd.affine_select(out=mk[:, 1, :], in_=mk[:, 1, :], compare_op=ALU.is_ge, fill=-BIG, base=0,
                                    pattern=[[-1, P]], channel_multiplier=1).then_inc(const_ready, 1)

        @block.scalar
        def _(act):
            act.wait_ge(c_in, 16)
            nc.scalar.activation(cs[:], ct[:], ACT.Silu).then_inc(silu_done, 1)
            layer_norm_deviations(nc, act, T, eps, 0)

        @block.tensor
        def _(pe):
            pe.wait_ge(silu_done, 1)
            for n, m in enumerate((2, 5)):
                pe.wait_ge(wm_in[m], 16)
                for k in range(KT):
                    last = nc.tensor.matmul(bank[1][0:B, n, :], cs[:, k, :], wm[:, m, k, :], start=(k == 0), stop=(k == KT - 1))
            last.then_inc(g_done, 1)
            for n, m in enumerate((0, 1, 3, 4)):
                pe.wait_ge(wm_in[m], 16)
                for o in range(KT):
                    for k in range(KT):
                        last = nc.tensor.matmul(bank[0][:, 0, (n * KT + o) * B:(n * KT + o + 1) * B],
                                                wm[:, m, k, o * P:(o + 1) * P], cs[:, k, :],
                                                start=(k == 0), stop=(k == KT - 1))
            last.then_inc(mod_done, 1)

        @block.vector
        def _(dve):
            chain = Chain(dve, dve_step)
            nc.vector.memset(T["kst"][96:98, :].bitcast(F32), 1.0)
            nc.vector.memset(T["vs"][:, :, 2 * HD:3 * HD].bitcast(F32), 1.0)
            chain.link(nc.vector.memset(ones[:], 1.0))
            nc.vector.tensor_copy(T["ones"][:], ones[:])
            dve.wait_ge(g_done, 1)
            floored(nc, chain, gains[:].rearrange("b g n -> b (g n)"), bank[1][0:B].rearrange("b g n -> b (g n)"), fl, g_ready)
            for t in range(len(T["x_in"])):
                layer_norm_statistics(nc, dve, chain, T, eps, 0, t)
            for t in range(len(T["x_in"])):
                layer_norm_tile(nc, dve, chain, T, 0, t)
            dve.wait_ge(w_in, 96)
            chain.link(nc.vector.tensor_copy(qsp[:, 0], qraw[:]))
            nc.vector.tensor_tensor(qsp[:, 1], qraw[:], qsp[:, 0].bitcast(F32), ALU.subtract).then_inc(split_ready, 1)
            chain.link(nc.vector.tensor_copy(T["ow"][:, 0], oraw[:]))
            nc.vector.tensor_tensor(T["ow"][:, 1], oraw[:], T["ow"][:, 0].bitcast(F32), ALU.subtract)
            chain.link(nc.vector.tensor_copy(T["kvw"][:, 0], kvraw[:]))
            nc.vector.tensor_tensor(T["kvw"][:, 1], kvraw[:], T["kvw"][:, 0].bitcast(F32), ALU.subtract)
            dve.wait_ge(const_ready, 3)
            nc.vector.tensor_copy(T["identr"][:], ident[:])
            nc.vector.tensor_copy(T["mask_kq"][:], mk[:, 0, :])
            nc.vector.tensor_copy(T["mask_qk"][:], mk[:, 1, :])
            dve.wait_ge(mod_done, 1)
            src = bank[0][:, 0, 0:4 * KT * B].rearrange("p (m k b) -> p m k b", m=4, k=KT)
            for m, one in enumerate((0.0, 1.0, 0.0, 1.0)):
                nc.vector.tensor_scalar(mod[:, m], src[:, m], one, None, ALU.add)
            dve.wait_ge(bias_in, 80)
            chain.link(nc.vector.tensor_copy(obs[:, 0, :], obr[:]))
            nc.vector.tensor_tensor(obs[:, 1, :], obr[:], obs[:, 0, :].bitcast(F32), ALU.subtract).then_inc(ob_split, 1)


def floored(nc, chain, out, g, tmp, ready):
    chain.link(nc.vector.tensor_copy(tmp[:, 0, :], g))
    chain.link(nc.vector.tensor_scalar(tmp[:, 2, :], tmp[:, 0, :], 0.0, 2.0, ALU.is_ge, ALU.mult))
    nc.vector.tensor_scalar(tmp[:, 2, :], tmp[:, 2, :], 1.0, None, ALU.subtract)
    chain.link(nc.vector.scalar_tensor_tensor(out=tmp[:, 1, :], in0=tmp[:, 0, :], scalar=-1.0, in1=tmp[:, 0, :],
                                              op0=ALU.mult, op1=ALU.max))
    nc.vector.scalar_tensor_tensor(out=out, in0=tmp[:, 1, :], scalar=0.25, in1=tmp[:, 2, :],
                                   op0=ALU.max, op1=ALU.mult).then_inc(ready, 1)


def attention_phase(nc, io, B, S, sem, sb, bank, ident, mod, eps, T, qw_dram, inverse_dram, x1_dram):
    TT = S // P
    side, obank = bank[2], bank[3]

    def scores(n):
        return bank[n // 2][:, n % 2, :]

    ow, kvw, identr, kst, vs = T["ow"], T["kvw"], T["identr"], T["kst"], T["vs"]
    x, x_in, xn_ready = T["x"], T["x_in"], T["xn_ready"]
    modb = sb("mod_batch", [P, 2, KT, 1])
    xr = sb("x_residual", [P, 2, D])
    ht = sb("h_t_split", [P, 2, KT, S], F32R)
    pr = sb("probs", [P, RING, HALF])
    prs = [sb(f"probs_split{n}", [P, 2, HALF], F32R) for n in range(RING)]
    hs = pr[:]
    qw = sb("qw_group", [P, 2, KT, P], F32R)
    qb = sb("qb_group", [P, 1])
    qs = sb("q_split", [P, 2, S], F32R)
    qst = sb("q_stacks", [98, 4, S], F32R)
    kv = sb("kv", [P, S])
    m1, m2 = sb("max_first", [P, 8]), sb("max_second", [P, 4])
    nm = sb("neg_max", [P, 2 * 8], F32R)
    mr = sb("neg_max_rows", [16, 4, P], F32R)
    oraw = sb("o_raw", [2 * HD + 1, S])
    sums = sb("sums", [P, S // HD])
    og = sb("o_group", [P, 3, S])
    ot = sb("o_split", [P, 2, KT, S], F32R)
    x1 = sb("x1_out", [P, 2, D])
    tmp = sb("x1_tmp", [P, 1, D])

    x1_ready, xr_in = sem("x1_ready"), [sem("xr_in0"), sem("xr_in1")]
    x1_out = [sem(f"x1_out{n}") for n in range(2)]
    modb_ready, xt_done, h_ready = sem("modb_ready"), sem("xt_done"), sem("h_ready")
    ht_lo = [sem("ht_lo0"), sem("ht_lo1")]
    kst_ready, vt_done, vs_ready = sem("kst_ready"), sem("vt_done"), sem("vs_ready")
    qw_in, q_hi = sem("qw_in"), sem("q_hi")
    q_loaded = [sem(f"q_loaded{n}") for n in range(4)]
    m_loaded = [sem(f"m_loaded{n}") for n in range(4)]
    side_full, side_free = [sem("side_full0"), sem("side_full1")], [sem("side_free0"), sem("side_free1")]
    nm_ready, scored, exped = sem("nm_ready"), sem("scored"), sem("exped")
    sums_inverted, inverse_out, inverse_in = sem("sums_inverted"), sem("inverse_out"), sem("inverse_in")
    lo_dve, lo_pool, o_summed, vs_lo = sem("lo_dve"), sem("lo_pool"), sem("o_summed"), sem("vs_lo")
    pv_done, o_free = sem("pv_done"), [sem("o_free0"), sem("o_free1")]
    gathered, group_normed = sem("gathered"), sem("group_normed")
    dve_step = sem("attn_dve_step")

    def lo_count(head, u, on_pool):
        return head * ON_POOL.count(on_pool) + ON_POOL[:u + 1].count(on_pool)

    def side_use(b, n, g=0):
        return n % 2, (n - SIDE_FIRST) // 2 + b * (SIDE_ALL // 2) + g * (SIDE_PER_PASS // 2)

    def side_of_max(n, i):
        return SIDE_STEP[n] + 2 * (n in Q_STEPS) + i

    def side_taken(engine, b, n, g=0):
        r, use = side_use(b, n, g)
        engine.wait_ge(side_free[r], use + 1)

    class Edge:

        def __init__(self, b, has_next):
            self.prev, self.next = b, (0 if b is None else b + 1) if has_next else None
            self.side_b = 0 if b is None else b
            self.order = edge_order(b is not None, has_next)
            self.first = SIDE_FIRST if b is None else SIDE_EDGE

        def side(self, *key):
            return self.first + self.order.index(key)

    def all_steps(engine, step, b, chain=None, per_pass=0):
        for n in FIRST_STEPS:
            step(b, n, 0)
        with engine.Fori(0, PASSES) as g:
            if chain:
                inner = chain.loop(g, per_pass)
            for n in LOOP_STEPS:
                step(b, n, g)
            if chain:
                chain.end(inner, PASSES)
        for n in LAST_STEPS:
            step(b, n, 0)

    def batches(engine, batch, edge, chain=None, per_batch=0):
        edge(Edge(None, True))
        with engine.Fori(0, B - 1) as b:
            if chain:
                outer = chain.loop(b, per_batch)
            batch(b, True)
            edge(Edge(b, True))
            if chain:
                chain.end(outer, B - 1)
        batch(B - 1, False)
        edge(Edge(B - 1, False))

    with nc.Block() as block:
        @block.sync
        def _(sp):
            def fetch_group(group):
                sp.dma_start(qw[:].bitcast(F32), qw_dram[group]).then_inc(qw_in, 16)
                sp.dma_start(qb[:], io["qb"][group]).then_inc(qw_in, 16)

            def load_stack(b, n, g):
                s = n % 4
                sp.wait_ge(scored, (b * HEADS + 4 * g + n - 3) * NU if n >= 3 else b * HEADS * NU)
                for part, of in enumerate((0, 0, 1)):
                    sp.dma_start(qst[part * HD:(part + 1) * HD, s, :].bitcast(F32), qs[s * HD:(s + 1) * HD, of, :].bitcast(F32)).then_inc(q_loaded[s], 16)

            def load_max(b, n, side_b, side_n, g):
                s = n % 4
                side_taken(sp, side_b, side_n, g)
                sp.dma_start(qst[96:98, s, :].bitcast(F32).rearrange("r (t q) -> r t q", q=P), mr[:, s, :].bitcast(F32)).then_inc(m_loaded[s], 16)

            def gather(b, n, g):
                j = n % 4
                for c in range(2):
                    sp.wait_ge(o_free[c], b * HEADS + 4 * g + n + 1)
                sp.dma_start(sums[j * HD:(j + 1) * HD, :], oraw[2 * HD:2 * HD + 1, :].rearrange("r (t q) -> r t q", q=S // HD)).then_inc(gathered, 16)
                if j == 0 and n:
                    sp.wait_ge(group_normed, b * GROUPS + g + n // 4)
                for part in range(2):
                    sp.dma_start(og[j * HD:(j + 1) * HD, part, :], oraw[part * HD:(part + 1) * HD, :]).then_inc(gathered, 16)

            def spread_inverses(b, group):
                sp.wait_ge(sums_inverted, b * GROUPS + group + 1)
                sp.dma_start(inverse_dram.rearrange("j (t q) -> (j t) q", q=S // HD), sums[:]).then_inc(inverse_out, 16)
                sp.wait_ge(inverse_out, 16 * (b * GROUPS + group + 1))
                for j in range(4):
                    sp.dma_start(og[j * HD:(j + 1) * HD, 2, :], inverse_dram[j:j + 1, :].to_broadcast([HD, S])).then_inc(inverse_in, 16)

            def load_residual(b, t):
                sp.wait_ge(x1_ready, b * TT + TT + t - 1 if t > 1 else (b + 1) * TT)
                sp.dma_start(xr[:, t % 2, :], io["x"][b, t]).then_inc(xr_in[t % 2], 16)

            def step(b, n, g):
                if n in Q_STEPS:
                    side_taken(sp, b, SIDE_STEP[n] + 1, g)
                    fetch_group(g + (n + 3) // 4 + 1)
                if n == 0 or (n % 4 and n + 3 < HEADS):
                    load_stack(b, n + 3, g)
                if n <= LAST_MAX_STEP:
                    load_max(b, n + 2, b, side_of_max(n, NS - 1), g)
                if n % 4 == 3 and n + 4 < HEADS:
                    load_stack(b, n + 4, g)
                gather(b, n, g)
                if n % 4 == 3:
                    spread_inverses(b, g + n // 4)

            def batch(b, has_next):
                if has_next:
                    sp.wait_ge(xt_done, (b + 1) * 2 * KT)
                    for t in range(TT):
                        sp.dma_start(x[:, t, :], io["x"][b + 1, t]).then_inc(x_in[t], 16)
                for t in range(2):
                    load_residual(b, t)
                all_steps(sp, step, b)

            def edge(e):
                if e.next is not None:
                    side_taken(sp, e.side_b, e.side("q", 1))
                    for n in range(3):
                        load_stack(e.next, n, 0)
                    fetch_group(1)
                for t in range(TT):
                    if e.prev is not None:
                        sp.wait_ge(x1_ready, (e.prev + 1) * TT + t + 1)
                        sp.dma_start(x1_dram[e.prev, t], x1[:, t % 2, :]).then_inc(x1_out[t % 2], 16)
                        if t + 2 < TT:
                            load_residual(e.prev, t + 2)
                    if e.next is not None and t in (TT - 3, TT - 1):
                        n = (t == TT - 1) * 1
                        load_max(e.next, n, e.side_b, e.side("max", n, NS - 1), 0)

            fetch_group(0)
            batches(sp, batch, edge)
            for n in range(2):
                sp.wait_ge(x1_out[n], 16 * B * TT // 2)
            sp.wait_ge(qw_in, 32 * (B * GROUPS + 1))

        @block.scalar
        def _(act):
            def side_copy(b, n, g, out, bias, rows=P, width=HALF):
                r, use = side_use(b, n, g)
                act.wait_ge(side_full[r], use + 1)
                if bias is None:
                    ins = nc.scalar.activation(out, side[0:rows, r, 0:width], ACT.Copy)
                else:
                    ins = nc.scalar.activation(out, side[0:rows, r, 0:width], ACT.Identity, bias=bias)
                ins.then_inc(side_free[r], 1)

            def queries(b, group, h, side_b, side_n, g):
                r, use = side_use(side_b, side_n, g)
                if h == 0:
                    act.wait_ge(q_loaded[3], 48 * (b * GROUPS + group))
                act.wait_ge(side_full[r], use + 1)
                nc.scalar.activation(qs[:, 0, h * HALF:(h + 1) * HALF], side[:, r, :], ACT.Identity, bias=qb[:]).then_inc(q_hi, 1)

            def max_rows(n, side_b, side_n, g):
                side_copy(side_b, side_n, g, mr[:, n % 4, :], None, rows=16, width=P)

            def modulation(b):
                nc.scalar.activation(modb[:], mod[:, 0:2, :, bass.ds(b, 1)], ACT.Copy).then_inc(modb_ready, 1)

            def evacuate(b, n, g, c):
                head = b * HEADS + 4 * g + n
                act.wait_ge(pv_done, head * NU + (C0_UNITS, NU)[c])
                if c == 0:
                    act.wait_ge(gathered, 48 * head)
                nc.scalar.activation(oraw[:, c * HALF:(c + 1) * HALF], obank[0:2 * HD + 1, c, :], ACT.Copy).then_inc(o_free[c], 1)

            def step(b, n, g, has_next):
                if n in Q_STEPS:
                    for h in range(2):
                        queries(b, g + (n + 3) // 4, h, b, SIDE_STEP[n] + h, g)
                for u, (c, parts) in enumerate(UNITS):
                    unit = (b * HEADS + 4 * g + n) * NU + u
                    s = (n * NU + u) % RING
                    width = sum(p[2] for p in parts)
                    act.wait_ge(scored, unit + 1)
                    if n > 0 or u >= RING:
                        act.wait_ge(pv_done, unit - RING + 1)
                    ins = nc.scalar.activation(pr[:, s, 0:width], scores(s)[:, 0:width], ACT.Exp, scale=SCALE)
                    if ON_POOL[u]:
                        ins = nc.scalar.activation(prs[s][:, 0, 0:width], scores(s)[:, 0:width], ACT.Exp, scale=SCALE)
                    ins.then_inc(exped, 1)
                    if u == LAG and n > 0:
                        evacuate(b, n - 1, g, 1)
                    if u == NU - 2:
                        evacuate(b, n, g, 0)
                    if n == 15 and u == 0 and has_next:
                        modulation(b + 1)
                        layer_norm_deviations(nc, act, T, eps, b + 1)
                if n == 15:
                    evacuate(b, n, g, 1)
                if n <= LAST_MAX_STEP:
                    max_rows(n + 2, b, side_of_max(n, NS - 1), g)

            def batch(b, has_next):
                all_steps(act, lambda b, n, g: step(b, n, g, has_next), b)

            def edge(e):
                if e.next is None:
                    return
                if e.prev is None:
                    modulation(0)
                act.wait_ge(modb_ready, e.next + 1)
                for h in range(2):
                    for k in range(KT):
                        act.wait_ge(xt_done, e.next * 2 * KT + h * KT + k + 1)
                        if h:
                            act.wait_ge(ht_lo[0], e.next * KT + k + 1)
                        nc.scalar.activation(hs[:, k, :], scores(k), ACT.Identity, bias=modb[:, 0, k, :], scale=modb[:, 1, k, :])
                        nc.scalar.activation(ht[:, 0, k, h * HALF:(h + 1) * HALF], scores(k), ACT.Identity,
                                             bias=modb[:, 0, k, :], scale=modb[:, 1, k, :]).then_inc(h_ready, 1)
                for h in range(2):
                    side_copy(e.side_b, e.side("kv", h), 0, kv[:, h * HALF:(h + 1) * HALF], T["kvb"][:])
                    queries(e.next, 0, h, e.side_b, e.side("q", h), 0)
                max_rows(0, e.side_b, e.side("max", 0, NS - 1), 0)
                act.wait_ge(vt_done, e.next + 1)
                nc.scalar.activation(vs[:, :, 0:HD], obank[:, 0, 0:TT * HD].rearrange("p (t d) -> p t d", t=TT), ACT.Copy).then_inc(vs_ready, 1)
                max_rows(1, e.side_b, e.side("max", 1, NS - 1), 0)

            batches(act, batch, edge)

        @block.gpsimd
        def _(pool):
            def step(b, n, g):
                for u, (c, parts) in enumerate(UNITS):
                    if ON_POOL[u]:
                        head, s, width = b * HEADS + 4 * g + n, (n * NU + u) % RING, sum(p[2] for p in parts)
                        pool.wait_ge(exped, head * NU + u + 1)
                        nc.gpsimd.tensor_tensor(prs[s][:, 1, 0:width], pr[:, s, 0:width], prs[s][:, 0, 0:width].bitcast(F32),
                                                ALU.subtract).then_inc(lo_pool, 1)
                    if n % 4 == 0 and n and u in (NU - 3, NU - 1):
                        sum_parts(b, g + n // 4 - 1, (u == NU - 1) * 1)

            def sum_parts(b, group, half):
                at = slice(half * HALF, (half + 1) * HALF)
                pool.wait_ge(gathered, 48 * (b * HEADS + 4 * (group + 1)))
                nc.gpsimd.tensor_tensor(og[:, 0, at], og[:, 0, at], og[:, 1, at], ALU.add).then_inc(o_summed, 1)

            def batch(b, has_next):
                all_steps(pool, step, b)

            def edge(e):
                if e.next is not None:
                    for k in range(KT):
                        pool.wait_ge(h_ready, e.next * 2 * KT + KT + k + 1)
                        nc.gpsimd.tensor_tensor(ht[:, 1, k, HALF:S], hs[:, k, :], ht[:, 0, k, HALF:S].bitcast(F32),
                                                ALU.subtract).then_inc(ht_lo[1], 1)
                if e.prev is not None:
                    for half in range(2):
                        sum_parts(e.prev, GROUPS - 1, half)

            batches(pool, batch, edge)

        @block.vector
        def _(dve):
            chain = Chain(dve, dve_step)
            nc.vector.memset(tmp[:, 0, :], 0.0).then_inc(x1_ready, TT)

            def reduce_slot(side_b, side_n, g, i):
                r, use = side_use(side_b, side_n, g)
                dve.wait_ge(side_full[r], use + 1)
                for qt, k0, w, col in SLOTS[i]:
                    out = m1[:, qt:qt + 1] if k0 == 0 else m2[:, qt - 4:qt - 3]
                    last = nc.vector.tensor_reduce(out, side[:, r, col:col + w], AX.X, ALU.max)
                last.then_inc(side_free[r], 1)

            def merge_maxima(last_slots, last_transposed, side_b, g):
                for side_n in last_slots:
                    side_taken(dve, side_b, side_n, g)
                chain.link(nc.vector.tensor_tensor(m1[:, 4:8], m1[:, 4:8], m2[:], ALU.max))
                if last_transposed is not None:
                    r, use = side_use(side_b, last_transposed, g)
                    dve.wait_ge(side_full[r], use + 1)
                chain.link(nc.vector.tensor_scalar(nm[:, 0:8], m1[:], -1.0, None, ALU.mult))
                nc.vector.scalar_tensor_tensor(out=nm[:, 8:16], in0=m1[:], scalar=-1.0, in1=nm[:, 0:8].bitcast(F32),
                                               op0=ALU.mult, op1=ALU.subtract).then_inc(nm_ready, 1)

            def split_queries(b, group, h, side_b, side_n, g):
                r, use = side_use(side_b, side_n, g)
                dve.wait_ge(q_hi, 2 * (b * GROUPS + group) + h + 1)
                at = slice(h * HALF, (h + 1) * HALF)
                nc.vector.scalar_tensor_tensor(out=qs[:, 1, at], in0=side[:, r, :], scalar=qb[:], in1=qs[:, 0, at].bitcast(F32),
                                               op0=ALU.add, op1=ALU.subtract).then_inc(side_free[r], 1)

            def invert_sums(b, group):
                dve.wait_ge(gathered, 48 * (b * HEADS + 4 * (group + 1)))
                nc.vector.reciprocal(sums[:], sums[:]).then_inc(sums_inverted, 1)

            def normalise(piece, b, group, to):
                half, stage = divmod(piece, 3)
                at = slice(half * HALF, (half + 1) * HALF)
                if stage == 0:
                    if half == 0:
                        dve.wait_ge(inverse_in, 64 * (b * GROUPS + group + 1))
                    dve.wait_ge(o_summed, 2 * (b * GROUPS + group) + half + 1)
                    chain.link(nc.vector.tensor_tensor(og[:, 0, at], og[:, 0, at], og[:, 2, at], ALU.mult))
                elif stage == 1:
                    chain.link(nc.vector.tensor_copy(ot[:, 0, to, at], og[:, 0, at]))
                else:
                    last = nc.vector.tensor_tensor(ot[:, 1, to, at], og[:, 0, at], ot[:, 0, to, at].bitcast(F32), ALU.subtract)
                    if half:
                        last.then_inc(group_normed, 1)

            def step(b, n, g, has_next):
                if n in Q_STEPS:
                    for h in range(2):
                        split_queries(b, g + (n + 3) // 4, h, b, SIDE_STEP[n] + h, g)
                for u, (c, parts) in enumerate(UNITS):
                    if n <= LAST_MAX_STEP:
                        at = [side_of_max(n, i) for i in range(NS)]
                        for i, at_u in enumerate(SLOT_UNITS):
                            if at_u == u:
                                reduce_slot(b, at[i], g, i)
                        if u == SLOT_UNITS[-1] + 1:
                            merge_maxima(at[NS - 3:NS - 1], at[0] - (3 if n in Q_STEPS else 1), b, g)
                    if not ON_POOL[u]:
                        head, s, width = b * HEADS + 4 * g + n, (n * NU + u) % RING, sum(p[2] for p in parts)
                        dve.wait_ge(exped, head * NU + u + 1)
                        chain.link(nc.vector.tensor_copy(prs[s][:, 0, 0:width], pr[:, s, 0:width]))
                        nc.vector.tensor_tensor(prs[s][:, 1, 0:width], pr[:, s, 0:width], prs[s][:, 0, 0:width].bitcast(F32),
                                                ALU.subtract).then_inc(lo_dve, 1)
                    group = g + n // 4 - 1
                    if n % 4 == 0 and n and u == NU - 3:
                        invert_sums(b, group)
                    if n in NORM_STEPS:
                        for piece in NORM_PIECES.get(u, ()):
                            normalise(piece, b, group, group)
                    if has_next and n == 14 and u < TT:
                        layer_norm_statistics(nc, dve, chain, T, eps, b + 1, u)
                    if has_next and n == 15 and u >= NU - TT:
                        layer_norm_tile(nc, dve, chain, T, b + 1, u - (NU - TT))

            def batch(b, has_next):
                all_steps(dve, lambda b, n, g: step(b, n, g, has_next), b, chain, 12 + 4 * ON_POOL.count(False))

            def edge(e):
                if e.next is not None:
                    for k in range(KT):
                        dve.wait_ge(h_ready, e.next * 2 * KT + k + 1)
                        nc.vector.tensor_tensor(ht[:, 1, k, 0:HALF], hs[:, k, :], ht[:, 0, k, 0:HALF].bitcast(F32),
                                                ALU.subtract).then_inc(ht_lo[0], 1)
                if e.prev is not None:
                    invert_sums(e.prev, 3)
                if e.next is not None:
                    split_queries(e.next, 0, 0, e.side_b, e.side("q", 0), 0)
                if e.prev is not None:
                    for piece in range(6):
                        normalise(piece, e.prev, GROUPS - 1, GROUPS - 1)
                if e.next is not None:
                    split_queries(e.next, 0, 1, e.side_b, e.side("q", 1), 0)
                    side_taken(dve, e.side_b, e.side("kv", 1))
                    chain.link(nc.vector.tensor_copy(kst[0:96, :], kv[0:96, :]))
                    nc.vector.tensor_tensor(kst[32:64, :], kv[32:64, :], kst[32:64, :].bitcast(F32), ALU.subtract).then_inc(kst_ready, 1)
                for key in e.order:
                    if key[0] == "out":
                        project_tile(e, key[1])
                    elif key[0] == "max" and key[2] < NS - 1:
                        n, i = key[1:]
                        reduce_slot(e.side_b, e.side(*key), 0, i)
                        if i == NS - 2:
                            merge_maxima([e.side("max", n, NS - 3), e.side("max", n, NS - 2)],
                                         e.side("max", 0, NS - 1) if n else None, e.side_b, 0)
                    elif key[:2] == ("max", 0):
                        dve.wait_ge(vs_ready, e.next + 1)
                        nc.vector.tensor_tensor(vs[:, :, HD:2 * HD], obank[:, 0, 0:TT * HD].rearrange("p (t d) -> p t d", t=TT),
                                                vs[:, :, 0:HD].bitcast(F32), ALU.subtract).then_inc(vs_lo, 1)

            def project_tile(e, t):
                r, use = side_use(e.side_b, e.side("out", t))
                dve.wait_ge(side_full[r], use + 1)
                nc.vector.tensor_tensor(tmp[:, 0, :], side[:, r, :], T["ga"][:, e.prev, :], ALU.mult).then_inc(side_free[r], 1)
                dve.wait_ge(side_free[r], use + 1)
                dve.wait_ge(x1_out[t % 2], 16 * (e.prev * TT // 2 + t // 2))
                dve.wait_ge(xr_in[t % 2], 16 * (e.prev * TT // 2 + t // 2 + 1))
                nc.vector.tensor_tensor(x1[:, t % 2, :], tmp[:, 0, :], xr[:, t % 2, :], ALU.add).then_inc(x1_ready, 1)
                dve.wait_ge(x1_ready, (e.prev + 1) * TT + t + 1)

            batches(dve, batch, edge, chain, 51 + HEADS * ON_POOL.count(False))

        @block.tensor
        def _(pe):
            def side_bank(b, n, g=0):
                r, use = side_use(b, n, g)
                pe.wait_ge(side_free[r], use)
                return r

            def product(out, weights, moving, kts, last=True):
                for k in range(kts):
                    for a, m in ((0, 0), (0, 1), (1, 0)):
                        ins = nc.tensor.matmul(out, weights(a, k), moving(m, k), start=(k == 0 and a + m == 0),
                                               stop=(last and k == kts - 1 and a == 1))
                return ins

            def project_q(b, group, h, side_b, side_n, g):
                pe.wait_ge(qw_in, 32 * (b * GROUPS + group + 1))
                r = side_bank(side_b, side_n, g)
                product(side[:, r, :], lambda p, k: qw[:, p, k, :],
                        lambda p, k: ht[:, p, k, h * HALF:(h + 1) * HALF], KT).then_inc(side_full[r], 1)

            def max_slot(b, n, g, i, side_b, side_n):
                s = n % 4
                r = side_bank(side_b, side_n, g)
                if i == NS - 1:
                    pe.wait_ge(nm_ready, b * HEADS + 4 * g + n + 1)
                    nc.tensor.transpose(side[0:16, r, 0:P], nm[:].bitcast(F32), ident[:]).then_inc(side_full[r], 1)
                    return
                if i == 0:
                    pe.wait_ge(q_loaded[s], 48 * (b * GROUPS + g + n // 4 + 1))
                for qt, k0, w, col in SLOTS[i]:
                    diagonal = k0 + w == (qt + 1) * P
                    last = nc.tensor.matmul(side[:, r, col:col + w], qst[0:96, s, qt * P:(qt + 1) * P], kst[0:96, k0:k0 + w],
                                            start=True, stop=not diagonal)
                    if diagonal:
                        last = nc.tensor.matmul(side[:, r, col + w - P:col + w], identr[:], T["mask_qk"][:],
                                                start=False, stop=True)
                last.then_inc(side_full[r], 1)

            def score(b, n, g, u):
                s = n % 4
                unit = (b * HEADS + 4 * g + n) * NU + u
                if u == 0:
                    pe.wait_ge(m_loaded[s], 16 * (b * GROUPS + g + n // 4 + 1))
                if n > 0 or u >= RING:
                    pe.wait_ge(exped, unit - RING + 1)
                out = scores((n * NU + u) % RING)
                for kt, q0, w, col in UNITS[u][1]:
                    diagonal = q0 == kt * P
                    last = nc.tensor.matmul(out[:, col:col + w], kst[0:98, kt * P:(kt + 1) * P], qst[0:98, s, q0:q0 + w],
                                            start=True, stop=not diagonal)
                    if diagonal:
                        last = nc.tensor.matmul(out[:, col:col + P], identr[:], T["mask_kq"][:], start=False, stop=True)
                last.then_inc(scored, 1)

            def weigh(b, n, g, u):
                c, parts = UNITS[u]
                head, s = b * HEADS + 4 * g + n, (n * NU + u) % RING
                pe.wait_ge(lo_pool if ON_POOL[u] else lo_dve, lo_count(head, u, ON_POOL[u]))
                if parts[0][0] == 0 and (n > 0 or c == 0):
                    pe.wait_ge(o_free[c], head)
                for kt, q0, w, col in parts:
                    for part in range(2):
                        ins = nc.tensor.matmul(obank[0:3 * HD, c, q0 - c * HALF:q0 - c * HALF + w], vs[:, kt, :],
                                               prs[s][:, part, col:col + w], start=(kt == 0 and part == 0),
                                               stop=(kt == UNITS[(C0_UNITS, NU)[c] - 1][1][-1][0] and part == 1))
                ins.then_inc(pv_done, 1)

            def weigh_late(b, n, g, u):
                if u >= LAG:
                    weigh(b, n, g, u - LAG)
                elif n > 0:
                    weigh(b, n - 1, g, u - LAG + NU)

            def step(b, n, g):
                if n in Q_STEPS:
                    for h in range(2):
                        project_q(b, g + (n + 3) // 4, h, b, SIDE_STEP[n] + h, g)
                for u in range(NU):
                    score(b, n, g, u)
                    weigh_late(b, n, g, u)
                    if n <= LAST_MAX_STEP:
                        for i, at in enumerate(SLOT_UNITS):
                            if at == u:
                                max_slot(b, n + 2, g, i, b, side_of_max(n, i))
                if n == HEADS - 1:
                    for u in range(NU - LAG, NU):
                        weigh(b, n, g, u)
                if n <= LAST_MAX_STEP:
                    max_slot(b, n + 2, g, NS - 1, b, side_of_max(n, NS - 1))

            def batch(b, has_next):
                pe.wait_ge(vs_lo, b + 1)
                all_steps(pe, step, b)

            def edge(e):
                if e.next is not None:
                    for h in range(2):
                        pe.wait_ge(xn_ready, e.next * TT + (h + 1) * TT // 2)
                        for k in range(KT):
                            if h:
                                pe.wait_ge(h_ready, e.next * 2 * KT + k + 1)
                            for t in range(TT // 2):
                                last = nc.tensor.transpose(scores(k)[:, t * P:(t + 1) * P],
                                                           x[:, h * TT // 2 + t, k * P:(k + 1) * P], ident[:])
                            last.then_inc(xt_done, 1)
                for key in e.order:
                    if key[0] == "kv":
                        h = key[1]
                        pe.wait_ge(ht_lo[h], (e.next + 1) * KT)
                        r = side_bank(e.side_b, e.side(*key))
                        product(side[:, r, :], lambda p, k: kvw[:, p, k, :],
                                lambda p, k: ht[:, p, k, h * HALF:(h + 1) * HALF], KT).then_inc(side_full[r], 1)
                    elif key[0] == "q":
                        project_q(e.next, 0, key[1], e.side_b, e.side(*key), 0)
                    elif key[0] == "out":
                        t = key[1]
                        if t == 0:
                            pe.wait_ge(group_normed, (e.prev + 1) * GROUPS)
                        r = side_bank(e.side_b, e.side(*key))
                        product(side[:, r, :], lambda p, k: ot[:, p, k, t * P:(t + 1) * P],
                                lambda p, k: ow[:, p, k, :], KT, last=False)
                        nc.tensor.matmul(side[:, r, :], T["ones"][:], T["ob"][:], start=False, stop=True).then_inc(side_full[r], 1)
                    else:
                        n, i = key[1:]
                        if (n, i) == (0, 0):
                            pe.wait_ge(kst_ready, e.next + 1)
                        if (n, i) == (0, NS - 1):
                            side_taken(pe, e.side_b, e.side("kv", 1))
                            pe.wait_ge(o_free[0], e.next * HEADS)
                        max_slot(e.next, n, 0, i, e.side_b, e.side(*key))
                        if (n, i) == (0, NS - 1):
                            for t in range(TT):
                                last = nc.tensor.transpose(obank[:, 0, t * HD:(t + 1) * HD], kv[96:P, t * P:(t + 1) * P], ident[96:P, 96:P])
                            last.then_inc(vt_done, 1)

            batches(pe, batch, edge)


def load_x1(pool, W, x1_dram, b, h):
    NT = HALF // P
    pool.dma_start(W["x1"][:, h], x1_dram[b, NT * h:NT * (h + 1)].rearrange("t p n -> p t n")).then_inc(W["x1_in"][h], 16)


def ffn_setup(nc, io, B, sem, sb, bank, W, gains_dram, x1_dram):
    had = sb("hadamard", [P, P])
    su = sb("signs", [P, KT + FT])
    but, but_pool = sb("butterfly", [P, KT * HALF]), sb("butterfly_pool", [P, KT * HALF])
    wsd = sb("wscale_down", [P, D])
    CH = 2 * FF // HALF
    small_in, gb_in = sem("ffn_small_in"), sem("gb_in")
    ug_in, d_in = [sem(f"ug_in{n}") for n in range(CH)], sem("down_in")
    su_ready, crossed, crossed_pool, folded, evacuated = (
        sem(n) for n in ("su_ready", "crossed", "crossed_pool", "folded", "evacuated"))
    dve_step, pool_step = sem("ffn_setup_step"), sem("ffn_setup_pool_step")
    down, upgate = W["d"], W["ug"]
    folds = [("ug", c) for c in range(6)] + [("down", 0), ("ug", 6), ("ug", 7), ("down", 1), ("down", 2), ("down", 3)]
    by_pool = [("down", 0), ("down", 1)]
    by_dve = [f for f in folds if f not in by_pool]

    def chunk(c):
        return upgate[:, :, c * HALF // FF, c * HALF % FF:c * HALF % FF + HALF]

    def tiles(fold):
        kind, c = fold
        if kind == "ug":
            return [(chunk(c)[:, k, :], [(chunk(c)[:, k, :], slice(0, HALF), k)]) for k in range(KT)]
        at = slice(c * P, (c + 1) * P)
        return [(down[:, f:f + 4, at], [(down[:, f + i, at], slice(i * P, (i + 1) * P), KT + f + i) for i in range(4)])
                for f in range(0, FT, 4)]

    def butterflies(engine, chain, fold, scratch, done, count):
        kind, c = fold
        if kind == "ug":
            w, t, stages = chunk(c), scratch[:].rearrange("p (k n) -> p k n", n=HALF), 2
        else:
            w, t, stages = down[:, :, c * P:(c + 1) * P], scratch[:].rearrange("p (f n) -> p f n", n=P), 4
        for stage in range(stages):
            a, z = (w, t) if stage % 2 == 0 else (t, w)
            i, o = (v.rearrange("p (a two h) n -> p a two h n", two=2, h=2 ** stage) for v in (a, z))
            engine.tensor_tensor(o[:, :, 0], i[:, :, 0], i[:, :, 1], ALU.add)
            last = engine.tensor_tensor(o[:, :, 1], i[:, :, 0], i[:, :, 1], ALU.subtract)
            if stage < stages - 1:
                chain.link(last)
        last.then_inc(done, 1)
        chain.engine.wait_ge(done, count)

    with nc.Block() as block:
        @block.sync
        def _(sp):
            def load_chunk(c):
                src = io["w_up"] if c < CH // 2 else io["w_gate"]
                at = c * HALF % FF
                sp.dma_start(chunk(c), src.rearrange("(k p) n -> p k n", p=P)[:, :, at:at + HALF]).then_inc(ug_in[c], 16)

            load_chunk(0)
            sp.dma_start(had[:], io["had"]).then_inc(small_in, 16)
            sp.dma_start(su[:, 0:KT], io["su_ug"]).then_inc(small_in, 16)
            sp.dma_start(su[:, KT:], io["su_dp"]).then_inc(small_in, 16)
            load_chunk(1)
            load_chunk(2)
            sp.dma_start(down[:], io["w_down"].rearrange("(f p) n -> p f n", p=P)).then_inc(d_in, 16)
            for c in range(3, CH):
                load_chunk(c)
            sp.dma_start(W["sug"][:], io["ws_ug"]).then_inc(gb_in, 16)
            sp.dma_start(wsd[:], io["ws_dp"].to_broadcast([P, D])).then_inc(gb_in, 16)
            sp.dma_start(W["gbw"][:], gains_dram[1:2].to_broadcast([P, B, D])).then_inc(gb_in, 16)
            sp.wait_ge(gb_in, 48)

        @block.gpsimd
        def _(pool):
            for h in range(2):
                load_x1(pool, W, x1_dram, 0, h)
            pool.wait_ge(d_in, 16)
            chain = Chain(pool, pool_step)
            for n, fold in enumerate(by_pool):
                butterflies(nc.gpsimd, chain, fold, but_pool, crossed_pool, n + 1)

        @block.scalar
        def _(act):
            act.wait_ge(su_ready, 1)
            n = 0
            for fold in folds:
                for _, parts in tiles(fold):
                    act.wait_ge(folded, n + 1)
                    for to, columns, s in parts:
                        last = nc.scalar.activation(to, bank[n % 4 // 2][:, n % 2, columns], ACT.Copy, scale=su[:, s:s + 1])
                    last.then_inc(evacuated, 1)
                    n += 1

        @block.tensor
        def _(pe):
            pe.wait_ge(small_in, 48)
            n = 0
            for fold in folds:
                by, done = (by_pool, crossed_pool) if fold in by_pool else (by_dve, crossed)
                pe.wait_ge(done, by.index(fold) + 1)
                for operand, _ in tiles(fold):
                    if n >= 4:
                        pe.wait_ge(evacuated, n - 3)
                    nc.tensor.matmul(bank[n % 4 // 2][:, n % 2, :], had[:], operand, start=True, stop=True).then_inc(folded, 1)
                    n += 1

        @block.vector
        def _(dve):
            chain = Chain(dve, dve_step)
            for n, fold in enumerate(by_dve):
                if fold[0] == "ug":
                    dve.wait_ge(ug_in[fold[1]], 16)
                else:
                    dve.wait_ge(d_in, 16)
                butterflies(nc.vector, chain, fold, but, crossed, n + 1)
                if n == 0:
                    dve.wait_ge(small_in, 48)
                    nc.vector.tensor_scalar(su[:, 0:KT], su[:, 0:KT], float(D) ** -0.5, None, ALU.mult)
                    nc.vector.tensor_scalar(su[:, KT:], su[:, KT:], float(FF) ** -0.5, None, ALU.mult).then_inc(su_ready, 1)
            dve.wait_ge(gb_in, 48)
            nc.vector.tensor_tensor(W["gbw"][:], W["gbw"][:], wsd[:].unsqueeze(1).to_broadcast([P, B, D]), ALU.mult)


def ffn_phase(nc, io, B, S, sem, sb, bank, ident, mod, eps, W, x1_dram):
    NT = HALF // P
    up, gate, acc = bank[0], bank[1], (bank[2], bank[3])
    modb = sb("mod_batch2", [P, 2, KT, 1])
    x1, x1_in = W["x1"], W["x1_in"]
    xn = sb("x1_normed", [P, NT, D])
    hs = sb("h2_t", [P, KT, HALF])
    ht = sb("h2_t_split", [P, 2, KT, HALF], F32R)
    wr = [[sb(f"w_ring{n}_{p}", [P, KT, 2, P], F32R) for p in range(2)] for n in range(2)]
    dr = [[sb(f"d_ring{n}_{p}", [P, D], F32R) for p in range(2)] for n in range(2)]
    sg = sb("silu_gate", [P, 2, HALF])
    y = sb("y", [P, HALF])
    ys = [sb(f"y_split{n}", [P, 2, HALF], F32R) for n in range(2)]
    out_sb, tmp = sb("out_sb", [P, 2, D]), sb("out_tmp", [P, 2, D])
    st6, mv, rs = sb("ln2_stats", [P, NT, 6]), sb("ln2_mean_var", [P, NT, 2]), sb("ln2_rstd", [P, 2, NT])

    stats_ready, sd_ready, xn_ready, xt_done, h_ready, ht_ready = (
        sem(n) for n in ("stats2_ready", "sd2_ready", "xn2_ready", "xt2_done", "h2_ready", "ht2_ready"))
    ug_cast, d_cast, ug_ready, d_ready = sem("ug_cast"), sem("d_cast"), sem("ug_ready"), sem("d_ready")
    ug_done, silu_done, y_mul, y_ready, d_done = sem("ug_done"), sem("silu_done"), sem("y_mul"), sem("y_ready"), sem("d_done")
    out_ready, stored, dve_step = sem("out_ready"), [sem("stored0"), sem("stored1")], sem("ffn_dve_step")
    PAIRS = FT // 2

    def at_tile(n):
        return n if isinstance(n, int) else bass.ds(n, 1)

    def pairs(engine, body, chain=None, per_pass=0):
        body(0, True, False)
        with engine.Fori(1, PAIRS - 1) as p:
            if chain:
                inner = chain.loop(p - 1, per_pass)
            body(p, False, False)
            if chain:
                chain.end(inner, PAIRS - 2)
        body(PAIRS - 1, False, True)

    def h_bank(k):
        return bank[k % 2][:, k // 2, :]

    def blocks(engine, block_of, chain=None, per_batch=0):
        with engine.Fori(0, B - 1) as b:
            if chain:
                outer = chain.loop(b, per_batch)
            block_of(b, 0, True)
            block_of(b, 1, True)
            if chain:
                chain.end(outer, B - 1)
        block_of(B - 1, 0, True)
        block_of(B - 1, 1, False)

    with nc.Block() as block:
        @block.gpsimd
        def _(pool):
            with pool.Fori(1, B) as b:
                for h in range(2):
                    pool.wait_ge(out_ready, (2 * b + h + 1) * NT)
                    load_x1(pool, W, x1_dram, b, h)

        @block.sync
        def _(sp):
            with sp.Fori(0, B) as b:
                for t in range(2 * NT):
                    sp.wait_ge(out_ready, (b + 1) * 2 * NT + t + 1)
                    sp.dma_start(io["out"][b, t], out_sb[:, t % 2, :]).then_inc(stored[t % 2], 16)
            for n in range(2):
                sp.wait_ge(stored[n], 16 * B * NT)

        @block.scalar
        def _(act):
            def deviations(b, blk):
                nc.scalar.activation(modb[:], mod[:, 2:4, :, at_tile(b)], ACT.Copy)
                act.wait_ge(stats_ready, blk + 1)
                nc.scalar.activation(rs[:, 0, :], mv[:, :, 1], ACT.Sqrt, bias=eps[:]).then_inc(sd_ready, 1)

            def modulate(blk, ks):
                for k in ks:
                    act.wait_ge(xt_done, blk * KT + k + 1)
                    nc.scalar.activation(hs[:, k, :], h_bank(k), ACT.Identity,
                                         bias=modb[:, 0, k, :], scale=modb[:, 1, k, :]).then_inc(h_ready, 1)

            def cast_ug(f, s, at):
                act.wait_ge(ug_done, f - 1)
                nc.scalar.activation(wr[s][0][:], W["ug"][:, :, :, bass.ds(at * P, P)], ACT.Copy).then_inc(ug_cast, 1)

            nc.scalar.activation(wr[0][0][:], W["ug"][:, :, :, 0:P], ACT.Copy).then_inc(ug_cast, 1)
            nc.scalar.activation(dr[0][0][:], W["d"][:, 0, :], ACT.Copy).then_inc(d_cast, 1)
            deviations(0, 0)
            modulate(0, range(KT))

            def block_of(b, h, has_next):
                blk = 2 * b + h

                def body(p, first, last):
                    for e in range(2):
                        f, s = blk * FT + 2 * p + e, e
                        ends = last and e == 1
                        at = 0 if ends else 2 * p + e + 1
                        if has_next or not ends:
                            cast_ug(f + 1, 1 - s, at)
                        act.wait_ge(ug_done, f + 1)
                        nc.scalar.activation(sg[:, s, :], gate[:, s, :], ACT.Silu,
                                             scale=W["sug"][:, 1, bass.ds(2 * p + e, 1)]).then_inc(silu_done, 1)
                        if has_next and ends:
                            modulate(blk + 1, (0, 1))
                        if has_next or not ends:
                            act.wait_ge(d_done, f)
                            nc.scalar.activation(dr[1 - s][0][:], W["d"][:, at_tile(at), :], ACT.Copy).then_inc(d_cast, 1)
                    if has_next and first:
                        deviations(b + h, blk + 1)
                    if has_next and last:
                        modulate(blk + 1, (2, 3))
                pairs(act, body)
            blocks(act, block_of)

        @block.vector
        def _(dve):
            chain = Chain(dve, dve_step)
            nc.vector.memset(tmp[:, 0, :], 0.0).then_inc(out_ready, 2 * NT)

            def statistics(batch, half, blk):
                dve.wait_ge(x1_in[half], 16 * (batch + 1))
                for t in range(NT):
                    last = nc.vector.bn_stats(st6[:, t, :], x1[:, half, t, :])
                chain.link(last)
                nc.vector.memset(eps[:], EPS)
                for t in range(NT):
                    last = nc.vector.bn_aggr(mv[:, t, :], st6[:, t, :])
                last.then_inc(stats_ready, 1)

            def normalise(half, blk):
                dve.wait_ge(sd_ready, blk + 1)
                chain.link(nc.vector.reciprocal(rs[:, 1, :], rs[:, 0, :]))
                for t in range(NT):
                    last = nc.vector.tensor_scalar(xn[:, t, :], x1[:, half, t, :], mv[:, t, 0:1], rs[:, 1, t:t + 1],
                                                   ALU.subtract, ALU.mult)
                last.then_inc(xn_ready, 1)

            def split_h(blk, ks):
                for k in ks:
                    dve.wait_ge(h_ready, blk * KT + k + 1)
                    chain.link(nc.vector.tensor_copy(ht[:, 0, k, :], hs[:, k, :]))
                    nc.vector.tensor_tensor(ht[:, 1, k, :], hs[:, k, :], ht[:, 0, k, :].bitcast(F32),
                                            ALU.subtract).then_inc(ht_ready, 1)

            def split_ug(f, s, at):
                dve.wait_ge(ug_cast, f + 1)
                nc.vector.tensor_tensor(wr[s][1][:], W["ug"][:, :, :, bass.ds(at * P, P)], wr[s][0][:].bitcast(F32),
                                        ALU.subtract).then_inc(ug_ready, 1)

            def split_d(f, s, at):
                dve.wait_ge(d_cast, f + 1)
                nc.vector.tensor_tensor(dr[s][1][:], W["d"][:, at_tile(at), :], dr[s][0][:].bitcast(F32), ALU.subtract).then_inc(d_ready, 1)

            statistics(0, 0, 0)
            normalise(0, 0)
            split_ug(0, 0, 0)
            split_d(0, 0, 0)
            split_h(0, range(KT))

            def block_of(b, h, has_next):
                blk = 2 * b + h

                def body(p, first, last):
                    for e in range(2):
                        f, s = blk * FT + 2 * p + e, e
                        ends = last and e == 1
                        at = 0 if ends else 2 * p + e + 1
                        if has_next or not ends:
                            split_ug(f + 1, 1 - s, at)
                        if not (isinstance(b, int) and b == 0 and h == 0 and first and e == 0):
                            dve.wait_ge(y_ready, f)
                        dve.wait_ge(silu_done, f + 1)
                        ins = nc.vector.scalar_tensor_tensor(out=y[:], in0=up[:, s, :], scalar=W["sug"][:, 0, bass.ds(2 * p + e, 1)],
                                                             in1=sg[:, s, :], op0=ALU.mult, op1=ALU.mult)
                        ins.then_inc(y_mul, 1)
                        dve.wait_ge(y_mul, f + 1)
                        if not first:
                            dve.wait_ge(d_done, f - 1)
                        chain.link(nc.vector.tensor_copy(ys[s][:, 0, :], y[:]))
                        nc.vector.tensor_tensor(ys[s][:, 1, :], y[:], ys[s][:, 0, :].bitcast(F32), ALU.subtract).then_inc(y_ready, 1)
                        if has_next and ends:
                            split_h(blk + 1, (0, 1))
                        if has_next or not ends:
                            split_d(f + 1, 1 - s, at)
                        if has_next and last and e == 0:
                            normalise(1 - h, blk + 1)
                    if has_next and first:
                        statistics(b + h, 1 - h, blk + 1)
                    if has_next and last:
                        split_h(blk + 1, (2, 3))
                pairs(dve, body, chain, 2)
                dve.wait_ge(d_done, (blk + 1) * FT)
                for t in range(NT):
                    chain.link(nc.vector.tensor_tensor(tmp[:, t % 2, :], acc[t // 2][:, t % 2, :], W["gbw"][:, b, :], ALU.mult))
                    dve.wait_ge(stored[t % 2], 16 * (blk * NT // 2 + t // 2))
                    ins = nc.vector.tensor_tensor(out_sb[:, t % 2, :], tmp[:, t % 2, :], x1[:, h, t, :], ALU.add)
                    ins.then_inc(out_ready, 1)
            blocks(dve, block_of, chain, 2 * (2 + KT + FT + NT))

        @block.tensor
        def _(pe):
            def transposes(blk, ks):
                pe.wait_ge(xn_ready, blk + 1)
                for k in ks:
                    for t in range(NT):
                        last = nc.tensor.transpose(h_bank(k)[:, t * P:(t + 1) * P], xn[:, t, k * P:(k + 1) * P], ident[:])
                    last.then_inc(xt_done, 1)

            def up_gate(f, s):
                pe.wait_ge(ug_ready, f + 1)
                for side in range(2):
                    for k in range(KT):
                        for a, m in ((0, 0), (0, 1), (1, 0)):
                            last = nc.tensor.matmul(bank[side][:, s, :], wr[s][a][:, k, side, :], ht[:, m, k, :],
                                                    start=(k == 0 and a + m == 0), stop=(k == KT - 1 and a == 1))
                last.then_inc(ug_done, 1)

            def down(f, s, first, last_one):
                pe.wait_ge(y_ready, f + 1)
                pe.wait_ge(d_ready, f + 1)
                for t in range(NT):
                    for a, m in ((0, 0), (0, 1), (1, 0)):
                        last = nc.tensor.matmul(acc[t // 2][:, t % 2, :], ys[s][:, a, t * P:(t + 1) * P], dr[s][m][:],
                                                start=(first and a + m == 0), stop=(last_one and a == 1))
                last.then_inc(d_done, 1)

            def block_of(b, h, has_next):
                blk = 2 * b + h
                pe.wait_ge(ht_ready, (blk + 1) * KT)

                def body(p, first, last):
                    f = blk * FT + 2 * p
                    for e in range(2):
                        if not first:
                            pe.wait_ge(y_mul, f + e - 1)
                        up_gate(f + e, e)
                        if has_next and last and e:
                            pe.wait_ge(y_mul, f + 1)
                            transposes(blk + 1, (0, 1))
                        if e:
                            if first:
                                pe.wait_ge(out_ready, (blk + 2) * NT)
                            down(f, 0, first, False)
                        elif not first:
                            down(f - 1, 1, False, False)
                    if has_next and last:
                        pe.wait_ge(y_mul, f + 2)
                        transposes(blk + 1, (2, 3))
                    if last:
                        down(f + 1, 1, False, True)
                pairs(pe, body)

            transposes(0, range(KT))
            blocks(pe, block_of)


def hadamard(n):
    import numpy as np
    return np.array([[1.0 - 2.0 * (bin(i & j).count("1") % 2) for j in range(n)] for i in range(n)], np.float32)


def kernel(**inputs):
    import numpy as np
    import concourse.bacc as bacc
    from concourse.bass_utils import run_bass_kernel_spmd

    a = {name.removeprefix("L0_"): np.asarray(v) for name, v in inputs.items()}
    x = a["attn_hidden_states"]
    B, S, _ = x.shape

    def lay(v):
        return np.ascontiguousarray(v)

    def columns(v):
        return lay(v.reshape(-1, P).T)

    arrays = dict(
        x=lay(x.reshape(B, S // P, P, D)),
        cT=lay(a["c"].T.reshape(KT, P, B).transpose(1, 0, 2)),
        wmod=lay(a["wmod"]),
        qwT=lay(a["attn_q_w"].T), kwT=lay(a["attn_k_w"].T), vwT=lay(a["attn_v_w"].T), owT=lay(a["attn_o_w"].T),
        qb=lay(np.concatenate([a["attn_q_b"], a["attn_q_b"][:P]]).reshape(GROUPS + 1, P, 1)), kb=lay(a["attn_k_b"].reshape(HD, 1)), vb=lay(a["attn_v_b"].reshape(HD, 1)),
        ob=lay(a["attn_o_b"].reshape(1, D)),
        su_ug=columns(a["ffn_SU_ug"]), su_dp=columns(a["ffn_SU_dp"]),
        ws_ug=lay(a["ffn_Wscale_ug"].reshape(2, FT, P).transpose(2, 0, 1)), ws_dp=lay(a["ffn_Wscale_dp"].reshape(1, D)),
        w_up=lay(a["ffn_W_up"].T), w_gate=lay(a["ffn_W_gate"].T), w_down=lay(a["ffn_W_down"].T),
        had=hadamard(P),
    )
    nc = bacc.Bacc("TRN2", target_bir_lowering=False, num_devices=1)
    io = {k: nc.dram_tensor(f"in_{k}", v.shape, mybir.dt.from_np(v.dtype), kind="ExternalInput").ap() for k, v in arrays.items()}
    io["out"] = nc.dram_tensor("out", (B, S // P, P, D), F32, kind="ExternalOutput").ap()
    program(nc, io, B, S)
    r = run_bass_kernel_spmd(nc, [{f"in_{k}": v for k, v in arrays.items()}], core_ids=[0])
    return r.results[0]["out"].reshape(B, S, D)
```
